# Optimizing a Trainium2 kernel written in Bass

```python
import numpy as np
import jax
import jax.numpy as jnp

def _softmax(x, axis=-1):
    return jax.nn.softmax(x, axis=axis)

def _gelu(x):
    return jax.nn.gelu(x, approximate=True)

def _silu(x):
    return jax.nn.silu(x)

def _sigmoid(x):
    return jax.nn.sigmoid(x)

def _layernorm(x, axis=-1, eps=1e-05):
    m = jnp.mean(x, axis=axis, keepdims=True)
    v = jnp.var(x, axis=axis, keepdims=True)
    return (x - m) / jnp.sqrt(v + eps)

def _scatter_add(tgt, idx, src, axis=0):
    return tgt.at[idx].add(src)

def _segment_sum(src, seg, n):
    return jax.ops.segment_sum(src, seg, n)
kernel_name = 'mk_decoder_preln_d1_seqx_r8_4b6805'

def setup_inputs(seed: int=0):
    np.random.seed(seed)
    _w = jnp.asarray

    def _rec_inputs():
        import jax
        import jax.numpy as jnp
        _rk = jax.random.key(seed)
        x = 7.22e-05 + 1 * jax.random.normal(jax.random.fold_in(_rk, 1), (4, 512, 128), jnp.float32)
        _lenS = 512 - jax.random.randint(jax.random.fold_in(_rk, 7), (4,), 0, max(1, 512 // 4) + 1, jnp.int32)
        _lenS2 = 77 - jax.random.randint(jax.random.fold_in(_rk, 8), (4,), 0, max(1, 77 // 4) + 1, jnp.int32)
        _ctx_1024P = jax.random.normal(jax.random.fold_in(_rk, 11), (4, 16, 128), jnp.float32)
        _ctx_1024c = jax.random.dirichlet(jax.random.fold_in(_rk, 511), 0.3 * jnp.ones((16,), jnp.float32), (4, 77))
        _ctx_1024t = jnp.einsum('bsk,bkd->bsd', _ctx_1024c, _ctx_1024P)
        _ctx_1024t = _ctx_1024t * jax.lax.rsqrt(jnp.mean(jnp.square(_ctx_1024t)) + 1e-12) * 0.953939
        ctx_1024 = 4.13588e-05 + 0.999923 * (_ctx_1024t + 0.3 * jax.random.normal(jax.random.fold_in(_rk, 611), (4, 77, 128), jnp.float32))
        _validS = jnp.arange(512)[None, :] < _lenS[:, None]
        _validS2 = jnp.arange(77)[None, :] < _lenS2[:, None]
        _causal = jnp.tril(jnp.ones((512, 512), dtype=bool))
        mask_Bx1x1xS2_bk0 = jnp.logical_not(jnp.broadcast_to(_validS2[:, None, None, :], (4, 1, 1, 77)))
        return (x, ctx_1024, mask_Bx1x1xS2_bk0)
    x, ctx_1024, mask_Bx1x1xS2_bk0 = _rec_inputs()

    def _L0_attn_setup():
        import jax, jax.numpy as jnp
        import numpy as np
        B, T, C = (2, 256, 128)
        N = 16
        D = C // N
        key = jax.random.key(seed)
        ks = jax.random.split(key, 5)
        s = 1.0 / np.sqrt(C)
        return {'x': jax.random.normal(ks[0], (B, T, C), dtype=jnp.float32), 'Wq': jax.random.normal(ks[1], (C, C), dtype=jnp.float32) * s, 'bq': jnp.zeros((C,), dtype=jnp.float32), 'Wk': jax.random.normal(ks[2], (C, C), dtype=jnp.float32) * s, 'bk': jnp.zeros((C,), dtype=jnp.float32), 'Wv': jax.random.normal(ks[3], (C, C), dtype=jnp.float32) * s, 'bv': jnp.zeros((C,), dtype=jnp.float32), 'Wp': jax.random.normal(ks[4], (C, C), dtype=jnp.float32) * s, 'bp': jnp.zeros((C,), dtype=jnp.float32)}
    _L0_attn_all = _L0_attn_setup()
    _L0_attn_in = {k: v for k, v in _L0_attn_all.items() if k in ('Wq', 'bq', 'Wk', 'bk', 'Wv', 'bv', 'Wp', 'bp')}
    del _L0_attn_all

    def _L0_xattn_setup():
        import jax, jax.numpy as jnp
        import numpy as np
        B, S, D, H = (4, 256, 128, 16)
        DH = D // H

        def _split_heads(x):
            b, s, _ = x.shape
            return x.reshape(b, s, H, DH).transpose(0, 2, 1, 3)
        key = jax.random.key(seed)
        ks = jax.random.split(key, 8)
        scale = 1.0 / np.sqrt(D)
        return {'query': jax.random.normal(ks[0], (B, S, D), jnp.float32), 'key': jax.random.normal(ks[1], (B, S, D), jnp.float32), 'value': jax.random.normal(ks[2], (B, S, D), jnp.float32), 'mask': jax.random.randint(ks[3], (B, 1, 1, S), 0, 2).astype(jnp.bool_), 'Wq': jax.random.normal(ks[4], (D, D), jnp.float32) * scale, 'Wk': jax.random.normal(ks[5], (D, D), jnp.float32) * scale, 'Wv': jax.random.normal(ks[6], (D, D), jnp.float32) * scale, 'Wo': jax.random.normal(ks[7], (D, D), jnp.float32) * scale}
    _L0_xattn_all = _L0_xattn_setup()
    _L0_xattn_in = {k: v for k, v in _L0_xattn_all.items() if k in ('Wq', 'Wk', 'Wv', 'Wo')}
    del _L0_xattn_all

    def _L0_ffn_setup():
        import jax, jax.numpy as jnp
        import numpy as np
        B, S, D, E, K = (4, 256, 128, 8, 2)
        EPS, W_THRES, TEMP = (0.0001, 0.1, 1.0)
        key = jax.random.key(seed)
        k1, k2, k3, k4, k5 = jax.random.split(key, 5)
        x = jax.random.normal(k1, (B, S, D), dtype=jnp.float32)
        gate_W = jax.random.normal(k2, (D, E), dtype=jnp.float32) * 0.02
        gate_b = jnp.zeros((E,), dtype=jnp.float32)
        expert_W = jax.random.normal(k3, (E, D, D), dtype=jnp.float32) * 0.02
        expert_b = jnp.zeros((E, D), dtype=jnp.float32)
        return {'x': x, 'gate_W': gate_W, 'gate_b': gate_b, 'expert_W': expert_W, 'expert_b': expert_b}
    _L0_ffn_all = _L0_ffn_setup()
    _L0_ffn_in = {k: v for k, v in _L0_ffn_all.items() if k in ('gate_W', 'gate_b', 'expert_W', 'expert_b')}
    del _L0_ffn_all
    return {'x': x, 'ctx_1024': ctx_1024, 'mask_Bx1x1xS2_bk0': mask_Bx1x1xS2_bk0, 'L0_attn_Wq': _L0_attn_in['Wq'], 'L0_attn_bq': _L0_attn_in['bq'], 'L0_attn_Wk': _L0_attn_in['Wk'], 'L0_attn_bk': _L0_attn_in['bk'], 'L0_attn_Wv': _L0_attn_in['Wv'], 'L0_attn_bv': _L0_attn_in['bv'], 'L0_attn_Wp': _L0_attn_in['Wp'], 'L0_attn_bp': _L0_attn_in['bp'], 'L0_xattn_Wq': _L0_xattn_in['Wq'], 'L0_xattn_Wk': _L0_xattn_in['Wk'], 'L0_xattn_Wv': _L0_xattn_in['Wv'], 'L0_xattn_Wo': _L0_xattn_in['Wo'], 'L0_ffn_gate_W': _L0_ffn_in['gate_W'], 'L0_ffn_gate_b': _L0_ffn_in['gate_b'], 'L0_ffn_expert_W': _L0_ffn_in['expert_W'], 'L0_ffn_expert_b': _L0_ffn_in['expert_b']}

def reference(x, ctx_1024, mask_Bx1x1xS2_bk0, L0_attn_Wq, L0_attn_bq, L0_attn_Wk, L0_attn_bk, L0_attn_Wv, L0_attn_bv, L0_attn_Wp, L0_attn_bp, L0_xattn_Wq, L0_xattn_Wk, L0_xattn_Wv, L0_xattn_Wo, L0_ffn_gate_W, L0_ffn_gate_b, L0_ffn_expert_W, L0_ffn_expert_b):
    import jax
    import jax.numpy as jnp

    def _L0_attn_ref(x, Wq, bq, Wk, bk, Wv, bv, Wp, bp):
        import jax, jax.numpy as jnp
        import numpy as np
        B, T, C = (2, 256, 128)
        N = 16
        D = C // N
        Bx, Tx, Cx = x.shape
        q = (x @ Wq + bq).reshape(Bx, Tx, N, D).transpose(0, 2, 1, 3)
        k = (x @ Wk + bk).reshape(Bx, Tx, N, D).transpose(0, 2, 1, 3)
        v = (x @ Wv + bv).reshape(Bx, Tx, N, D).transpose(0, 2, 1, 3)
        scores = jnp.einsum('bntd,bnsd->bnts', q, k) / jnp.sqrt(jnp.float32(D))
        causal = jnp.tril(jnp.ones((Tx, Tx), dtype=bool))
        scores = jnp.where(causal[None, None], scores, -jnp.inf)
        attn = jax.nn.softmax(scores, axis=-1)
        out = jnp.einsum('bnts,bnsd->bntd', attn, v)
        out = out.transpose(0, 2, 1, 3).reshape(Bx, Tx, Cx)
        return out @ Wp + bp

    def _L0_xattn_ref(query, key, value, mask, Wq, Wk, Wv, Wo):
        import jax, jax.numpy as jnp
        import numpy as np
        B, S, D, H = (4, 256, 128, 16)
        DH = D // H

        def _split_heads(x):
            b, s, _ = x.shape
            return x.reshape(b, s, H, DH).transpose(0, 2, 1, 3)
        q = _split_heads(query @ Wq.T)
        k = _split_heads(key @ Wk.T)
        v = _split_heads(value @ Wv.T)
        scores = jnp.einsum('bhqd,bhkd->bhqk', q, k) / np.sqrt(DH).astype(np.float32)
        scores = jnp.where(mask, jnp.float32(-1000000000.0), scores)
        attn = jax.nn.softmax(scores, axis=-1)
        ctx = jnp.einsum('bhqk,bhkd->bhqd', attn, v)
        ctx = ctx.transpose(0, 2, 1, 3).reshape(query.shape[0], -1, H * DH)
        return ctx @ Wo.T

    def _L0_ffn_ref(x, gate_W, gate_b, expert_W, expert_b):
        import jax, jax.numpy as jnp
        import numpy as np
        B, S, D, E, K = (4, 256, 128, 8, 2)
        EPS, W_THRES, TEMP = (0.0001, 0.1, 1.0)
        scores = jnp.maximum((x @ gate_W + gate_b) / TEMP, EPS)
        p = jax.nn.softmax(scores, axis=-1)
        _, topk_idx = jax.lax.top_k(p, K)
        topk_mask = jax.nn.one_hot(topk_idx, E, dtype=p.dtype).sum(-2) > 0
        w = jnp.maximum(p, W_THRES)
        w_gather = jnp.take_along_axis(w, topk_idx, axis=-1)
        total = jax.lax.stop_gradient(w_gather.sum(-1, keepdims=True))
        w = w / total
        comb = jnp.where(topk_mask, w, jnp.zeros_like(w))
        y = jnp.einsum('bsd,edf->bsef', x, expert_W) + expert_b
        out = jnp.einsum('bsef,bse->bsf', y, comb) / K
        return out
    x = x + _L0_attn_ref(_layernorm(x, axis=-1), L0_attn_Wq, L0_attn_bq, L0_attn_Wk, L0_attn_bk, L0_attn_Wv, L0_attn_bv, L0_attn_Wp, L0_attn_bp)
    x = x + _L0_xattn_ref(_layernorm(x, axis=-1), ctx_1024, ctx_1024, mask_Bx1x1xS2_bk0, L0_xattn_Wq, L0_xattn_Wk, L0_xattn_Wv, L0_xattn_Wo)
    x = x + _L0_ffn_ref(_layernorm(x, axis=-1), L0_ffn_gate_W, L0_ffn_gate_b, L0_ffn_expert_W, L0_ffn_expert_b)
    return x

_drawn_inputs = setup_inputs


def setup_inputs(seed=0):
    import zlib

    import numpy as np

    out = dict(_drawn_inputs(seed))
    spreads = {'L0_attn_bq': (0.0, 0.519),
     'L0_attn_bk': (0.0, 0.8),
     'L0_attn_bv': (0.0, 0.1),
     'L0_attn_bp': (0.0, 0.1),
     'L0_ffn_gate_b': (0.0, 0.1),
     'L0_ffn_expert_b': (0.0, 0.27)}
    factors = {}
    for name, (base, spread) in spreads.items():
        noise = np.random.default_rng([zlib.crc32(name.encode()), seed]).standard_normal(out[name].shape)
        drawn = base * np.exp(spread * noise) if base else spread * noise
        out[name] = jnp.asarray(drawn.astype(out[name].dtype))
    for name, factor in factors.items():
        out[name] = (out[name] * factor).astype(out[name].dtype)
    return out
```

```python
from contextlib import ExitStack

import numpy as np

import concourse.bass as bass
from concourse import mybir

F32 = mybir.dt.float32
BF16 = mybir.dt.bfloat16
U8 = mybir.dt.uint8
ALU = mybir.AluOpType
ACT = mybir.ActivationFunctionType
X_AXIS = mybir.AxisListType.X

B, S, D, H, E = 4, 512, 128, 16, 8
DH = D // H
S2 = 77
T = S // 128
PAIRS = H // 2
SCALE = float(1.0 / np.sqrt(np.float32(DH)))
MASKED = -1.0e9
FUTURE = -3.0e38
FLOOR, LEAST_WEIGHT, TOP_K = 1e-4, 0.1, 2
LN_EPS = 1e-5
VW = DH + 1

SLOT_ROWS = 6 * DH
MASK_ROW, MAX_ROW = 96, 122
Q_PARTS = (0, 0, 0, 1, 1, 2)
K_PARTS = (0, 1, 2, 0, 1, 0)
STACK_DMAS = 2 * len(Q_PARTS)

PEAKS = ([(0, [(p, None) for p in (2 * i, 2 * i + 1)]) for i in range(2)]
         + [(1, [(p, None)]) for p in range(4)]
         + [(t, [(p, s)]) for t in (2, 3) for p in range(4) for s in range(2)])
XPEAKS = [(t, h, n) for t in range(T) for h, n in ((0, 6), (6, 5), (11, 5))]
SCORES = [
    [(0, 0, 0, 0), (1, 0, 1, 0)],
    [(0, 0, 2, 0), (1, 0, 3, 0)],
    [(0, 0, 0, 3), (0, 128, 0, 1), (1, 0, 1, 3), (1, 128, 1, 1)],
    [(0, 0, 2, 3), (0, 128, 2, 1), (1, 0, 3, 3), (1, 128, 3, 1)],
    [(0, 0, 0, 2), (0, 256, 1, 2), (1, 0, 2, 2), (1, 256, 3, 2)],
]
PLACE = {(kt, j): (2 * u + bank, col) for u, unit in enumerate(SCORES) for bank, col, j, kt in unit}
VALUES = [((0,), 1), ((1, 3), 3), ((2,), 4)]


def spread(items, lo, hi):
    return [(lo + (hi - lo) * (i + 0.5) / len(items), x) for i, x in enumerate(items)]


def plan():
    def norm(b, n):
        return [("ln_stats", b, n), ("ln_norm", b, n), ("turn_x", b, n)]

    def prepare(b):
        return norm(b, 0) + [("project_q", b, 0), ("project_k", b, 0), ("split_q", b, 0), ("project_v", b, 0),
                             ("split_k", b, 0)]

    def peaks(b, f):
        return [("peak", b, (f, u)) for u in range(len(PEAKS))] + [("split_peaks", b, f), ("turn_peaks", b, f)]

    def attend(b, f):
        out = []
        for g in (2 * f, 2 * f + 1):
            s = [("scores", b, (g, u)) for u in range(5)]
            v = [("values", b, (g, v)) for v in range(3)]
            out += [s[0], s[1], s[2], v[0], s[3], s[4], v[1], v[2], ("take_mix", b, g), ("mix", b, g)]
        i, j = 7, 10
        return out[:i] + out[j:j + 2] + out[i:j] + out[j + 2:]

    def cross(b):
        out = [("turn_mix", b, 0), ("add_attention", b, 0)] + norm(b, 1) + [("project_xq", b, 0), ("split_xq", b, 0)]
        out += [("xpeak", b, u) for u in range(len(XPEAKS))] + [("split_xpeaks", b, 0), ("turn_xpeaks", b, 0)]
        out += [("xscores", b, 0)]
        for g in range(4):
            out += [("xscores", b, 2 * g + 1)] + [("xscores", b, 2 * g + 2)] * (g < 3)
            out += [("xvalues", b, g), ("xmix", b, g)]
        return out + [("turn_mix", b, 1), ("add_attention", b, 1)]

    def experts(b):
        out = norm(b, 2) + [("gate", b, 0), ("choose", b, 0), ("turn_gate", b, 0), ("expert_bias", b, 0)]
        return out + [("expert", b, t) for t in range(T)] + [("store", b, 0)]

    steps = prepare(0) + peaks(0, 0)
    for b in range(B):
        tail = cross(b - 1) + experts(b - 1) if b else []
        half = len(tail) // 2
        first = spread(attend(b, 0), 0, 1) + spread(peaks(b, 1), 0, 0.8)
        second = spread(attend(b, 1), 0, 1)
        if b + 1 < B:
            first += spread(prepare(b + 1), 0, 0.8)
            second += spread(peaks(b + 1, 0), 0, 0.8)
        if tail:
            first += spread(tail[:half], 0, 1)
            second += spread(tail[half:], 0, 1)
        for part in (first, second):
            steps += [x for _, x in sorted(part, key=lambda y: y[0])]
    return steps + cross(B - 1) + experts(B - 1)


SCHEDULE = plan()


def uses(*kinds):
    return {x: n + 1 for n, x in enumerate(x for x in SCHEDULE if x[0] in kinds)}


MISC = uses("turn_x", "project_q", "project_k", "project_v", "turn_peaks", "mix", "turn_mix",
            "add_attention", "project_xq", "turn_xpeaks", "xvalues", "xmix", "gate", "turn_gate", "expert_bias")
PAIR = uses("scores", "xscores", "expert")
PEAK = uses("peak", "xpeak")
MIX = uses("take_mix")
STATS = uses("ln_stats")
NORM = uses("ln_norm")
NORMS = list(NORM)
MISC_OF_ACT = ("turn_x", "project_q", "project_k", "project_xq", "turn_peaks", "turn_xpeaks", "turn_mix",
               "turn_gate", "xvalues")
MISC_OF_DVE = ("project_v", "mix", "xmix", "add_attention", "gate", "expert_bias")
MISC0 = 1 + B


def decoder_layer(nc, x, ctx_t, mask, wq, bq, wk, bk, wv, bv, wp, bp, xwq, xwk, xwv, xwo,
                  gate_w, gate_b, expert_w, expert_b, out):
    with ExitStack() as stack:
        def sb(name, shape, dt=F32):
            return stack.enter_context(nc.sbuf_tensor(name, shape, dt))

        def psum(name, shape):
            return stack.enter_context(nc.psum_tensor(name, shape, F32))

        def sem(name):
            return stack.enter_context(nc.semaphore(name))

        peak_ps = psum("peak_ps", [128, 2, 512])
        pair_ps = psum("pair_ps", [128, 2, 2, 512])
        mix_ps = psum("mix_ps", [128, 512])
        misc_ps = psum("misc_ps", [128, 512])

        wq_s, wk_s, wv_s, wp_s, xwq_s, xwk_s, xwv_s, xwo_s = (
            sb(n, [D, D]) for n in ("wq_s", "wk_s", "wv_s", "wp_s", "xwq_s", "xwk_s", "xwv_s", "xwo_s"))
        bq_s, bk_s = sb("bq_s", [D, 1]), sb("bk_s", [D, 1])
        bv_s, bp_s = sb("bv_s", [128, D]), sb("bp_s", [128, D])
        gate_w_s, gate_b_s = sb("gate_w_s", [D, E]), sb("gate_b_s", [128, E])
        expert_w_s = sb("expert_w_s", [D, E, D])
        expert_b_s = sb("expert_b_s", [T * E, T, D])
        ctx_s = sb("ctx_s", [D, B * S2])
        mask_s = sb("mask_s", [128, B * S2], U8)
        ident = sb("ident", [128, 128])
        ident_b = sb("ident_b", [128, 128], BF16)
        causal = sb("causal", [128, 4, 128], BF16)
        ones_b = sb("ones_b", [128, 512], BF16)
        minus_half = sb("minus_half", [128, T])
        rank = sb("rank", [128, T, E])
        keep = sb("keep", [128, B * S2])
        neg = sb("neg", [128, B * S2])
        neg_parts = sb("neg_parts", [128, 3, B * S2], BF16)

        state = sb("state", [128, B, T, D])
        stats = sb("stats", [128, 3 * B, T, 6])
        moments = sb("moments", [128, 3 * B, T, 2])
        var = sb("var", [128, 3 * B, T])
        rstd = sb("rstd", [128, 3 * B, T])
        normed = sb("normed", [128, 2, T, D])
        normed_t = [sb(f"normed_t{n}", [D, S]) for n in range(3)]

        kinds = ("q", "k", "x")
        full = {n: sb(f"full_{n}", [D, S]) for n in kinds}
        parts = {n: sb(f"parts_{n}", [D, 3, S], BF16) for n in kinds}
        q_stack = sb("q_stack", [128, 2, PAIRS, S], BF16)
        k_stack = sb("k_stack", [128, 2, 2, PAIRS, S], BF16)
        xq_stack = sb("xq_stack", [128, PAIRS, S], BF16)
        xk_stack = sb("xk_stack", [128, 2, PAIRS, B * S2], BF16)
        v_s = sb("v_s", [128, 2, T, H, VW])
        xv_s = sb("xv_s", [128, B, H, VW])

        peaks = sb("peaks", [128, 2, T, 4, 2])
        peak_rest = sb("peak_rest", [128, 2, T, 4, 2])
        peak_parts = sb("peak_parts", [128, 2, T, 2, 3, 4], BF16)
        peaks_t = sb("peaks_t", [24, 2, S], BF16)
        xpeaks = sb("xpeaks", [128, T, PAIRS, 2])
        xpeak_rest = sb("xpeak_rest", [128, T, PAIRS, 2])
        xpeak_parts = sb("xpeak_parts", [128, T, 2, 3, PAIRS], BF16)
        xpeaks_t = sb("xpeaks_t", [48, S], BF16)

        probs = sb("probs", [128, 2, 10, 512])
        xprobs = sb("xprobs", [128, 4, 512])
        mix_t = sb("mix_t", [128, 2, 512])
        share = sb("share", [128, 2, T, 4])
        mixed = sb("mixed", [128, 2, T, D])
        mixed_t = sb("mixed_t", [D, 2, S])

        g = {n: sb(f"g_{n}", [128, T, E]) for n in
             ("scores", "shifted", "exp", "p", "tied", "ranked", "first", "left", "tied2", "ranked2",
              "second", "chosen", "floored", "kept", "comb")}
        g1 = {n: sb(f"g1_{n}", [128, T]) for n in
              ("max", "sum", "inv", "top", "best", "top2", "best2", "total", "inv_total")}
        comb_t = sb("comb_t", [T * E, 128])
        yw = sb("yw", [128, 2, E, D])
        y4 = sb("y4", [128, 4, D])
        y2 = sb("y2", [128, 2, D])
        y1 = sb("y1", [128, D])

        x_loaded = [sem(f"x_loaded{b}") for b in range(B)]
        weights_loaded = sem("weights_loaded")
        zeroed = sem("zeroed")
        ones_stacked = sem("ones_stacked")
        mask_split = sem("mask_split")
        masks_stacked = sem("masks_stacked")
        var_ready, rstd_ready, norm_ready = sem("var_ready"), sem("rstd_ready"), sem("norm_ready")
        misc_full, misc_taken = sem("misc_full"), sem("misc_taken")
        pair_full = sem("pair_full")
        pair_taken = [sem("pair_taken0"), sem("pair_taken1")]
        peak_full, peak_taken = sem("peak_full"), sem("peak_taken")
        mix_cleared, mix_taken = sem("mix_cleared"), sem("mix_taken")
        rest_ready = {n: sem(f"rest_ready_{n}") for n in kinds}
        middle_ready = {n: sem(f"middle_ready_{n}") for n in kinds}
        low_ready = {n: sem(f"low_ready_{n}") for n in kinds}
        stacked = {n: [sem(f"stacked_{n}{i}") for i in range(2)] for n in kinds}
        xk_stacked = sem("xk_stacked")
        peaks_split, xpeaks_split = sem("peaks_split"), sem("xpeaks_split")
        max_stacked = [sem("max_stacked0"), sem("max_stacked1")]
        xmax_stacked = sem("xmax_stacked")
        causal_done = sem("causal_done")
        values_done = sem("values_done")
        shifted_ready, exp_ready, comb_ready = sem("shifted_ready"), sem("exp_ready"), sem("comb_ready")
        y_summed = sem("y_summed")
        stored = sem("stored")
        dve_chain, pool_chain = sem("dve_chain"), sem("pool_chain")

        block = stack.enter_context(nc.Block())

        WEIGHTS = [(wq_s, wq), (wk_s, wk), (wv_s, wv), (wp_s, wp), (xwq_s, xwq), (xwk_s, xwk), (xwv_s, xwv),
                   (xwo_s, xwo), (gate_w_s, gate_w), (bq_s, bq), (bk_s, bk), (ctx_s, ctx_t)]
        BROADCAST = [(bv_s, bv), (bp_s, bp), (gate_b_s, gate_b), (mask_s, mask)]
        N_WEIGHTS = len(WEIGHTS) + len(BROADCAST) + 1 + T
        N_ZEROED = 12
        N_ONES = 6 + 1
        PROJECTED = {"project_q": "q", "project_k": "k", "project_xq": "x"}
        SPLIT = {"split_q": "q", "split_k": "k", "split_xq": "x"}

        def wide(a):
            return a[:].unsqueeze(2).broadcast_to([128, T, E])

        def peak_bank(step):
            return peak_ps[:, PEAK[step] % 2, :]

        def pair_tile(step):
            return pair_ps[:, PAIR[step] % 2]

        @block.sync
        def _(sp):
            for b in range(B):
                sp.dma_start(state[:, b], x[b].rearrange("(t p) d -> p t d", p=128)).then_inc(x_loaded[b], 16)
                if b == 0:
                    for dst, src in WEIGHTS:
                        sp.dma_start(dst[:], src).then_inc(weights_loaded, 16)
                    for dst, src in BROADCAST:
                        sp.dma_start(dst[:], src.partition_broadcast(128)).then_inc(weights_loaded, 16)
            sp.wait_ge(zeroed, N_ZEROED)
            sp.dma_start(expert_w_s[:], expert_w.rearrange("e d f -> d e f")).then_inc(weights_loaded, 16)
            for t in range(T):
                sp.dma_start(expert_b_s[E * t:E * t + E, t, :], expert_b).then_inc(weights_loaded, 16)
            ones = ones_b[0:3 * PAIRS, :]
            for s in range(2):
                r = MAX_ROW + 3 * s
                for i in range(2):
                    sp.dma_start(k_stack[r:r + 3, i, s], ones).then_inc(ones_stacked, 16)
                sp.dma_start(xk_stack[r:r + 3, s], ones_b[0:3 * PAIRS, 0:B * S2]).then_inc(ones_stacked, 16)
            sp.dma_start(xq_stack[MASK_ROW:MASK_ROW + 3], ones).then_inc(ones_stacked, 16)
            sp.wait_ge(mask_split, 1)
            for s in range(2):
                for p in range(PAIRS):
                    sp.dma_start(xk_stack[MASK_ROW:MASK_ROW + 3, s, p],
                                 neg_parts[0:1]).then_inc(masks_stacked, 16)
            sp.wait_ge(low_ready["x"], 1)
            for i, part in enumerate(K_PARTS):
                for s in range(2):
                    r = SLOT_ROWS * s + DH * i
                    sp.dma_start(xk_stack[r:r + DH, s], parts["x"][64 * s:64 * s + 64, part, 0:B * S2]
                                 ).then_inc(xk_stacked, 16)

            for step in SCHEDULE:
                kind, b, k = step
                if kind in ("split_q", "split_k"):
                    n = SPLIT[kind]
                    sp.wait_ge(low_ready[n], b + 1)
                    if b >= 2:
                        sp.wait_ge(values_done, 12 * (b - 1))
                    for i, part in enumerate(Q_PARTS if n == "q" else K_PARTS):
                        for s in range(2):
                            r = SLOT_ROWS * s + DH * i
                            dst = q_stack[r:r + DH, b % 2] if n == "q" else k_stack[r:r + DH, b % 2, s]
                            sp.dma_start(dst, parts[n][64 * s:64 * s + 64, part, :]).then_inc(stacked[n][b % 2], 16)
                elif kind == "split_xq":
                    sp.wait_ge(low_ready["x"], b + 2)
                    if b >= 1:
                        sp.wait_ge(misc_full, MISC0 + MISC[("xvalues", b - 1, 3)])
                    for i, part in enumerate(Q_PARTS):
                        for s in range(2):
                            r = SLOT_ROWS * s + DH * i
                            sp.dma_start(xq_stack[r:r + DH], parts["x"][64 * s:64 * s + 64, part, :]
                                         ).then_inc(stacked["x"][b % 2], 16)
                elif kind == "turn_peaks":
                    sp.wait_ge(misc_taken, MISC0 + MISC[step])
                    for s in range(2):
                        r = MAX_ROW + 3 * s
                        sp.dma_start(q_stack[r:r + 3, b % 2, 4 * k:4 * k + 4],
                                     peaks_t[12 * s:12 * s + 12, k]).then_inc(max_stacked[k], 16)
                elif kind == "turn_xpeaks":
                    sp.wait_ge(misc_taken, MISC0 + MISC[step])
                    for s in range(2):
                        r = MAX_ROW + 3 * s
                        sp.dma_start(xq_stack[r:r + 3], xpeaks_t[24 * s:24 * s + 24, :]).then_inc(xmax_stacked, 16)
                elif kind == "store":
                    sp.wait_ge(y_summed, T * (b + 1))
                    sp.dma_start(out[b].rearrange("(t p) d -> p t d", p=128), state[:, b]).then_inc(stored, 16)
            sp.wait_ge(stored, 16 * B)

        @block.gpsimd
        def _(pool):
            gp = nc.gpsimd
            chain = [0]

            def link(ins):
                chain[0] += 1
                ins.then_inc(pool_chain, 1)
                pool.wait_ge(pool_chain, chain[0])

            link(gp.memset(ones_b[:], 1.0))
            link(gp.memset(ident[:], 0.0))
            link(gp.affine_select(out=ident[:], in_=ident[:], compare_op=ALU.not_equal, fill=1.0, base=0,
                                  pattern=[[-1, 128]], channel_multiplier=1))
            gp.tensor_copy(ident_b[:], ident[:]).then_inc(zeroed, 1)
            link(gp.memset(causal[:], 0.0))
            gp.affine_select(out=causal[:], in_=causal[:], compare_op=ALU.is_ge, fill=FUTURE, base=0,
                             pattern=[[0, 4], [-1, 128]], channel_multiplier=1).then_inc(zeroed, 1)
            gp.memset(minus_half[:], -0.5).then_inc(zeroed, 1)
            for e in range(E):
                last = gp.memset(rank[:, :, e:e + 1], float(E - e))
            last.then_inc(zeroed, 1)
            gp.memset(q_stack[:], 0.0).then_inc(zeroed, 1)
            gp.memset(k_stack[:], 0.0).then_inc(zeroed, 1)
            gp.memset(xq_stack[:], 0.0).then_inc(zeroed, 1)
            gp.memset(xk_stack[:], 0.0).then_inc(zeroed, 1)
            gp.memset(expert_b_s[:], 0.0).then_inc(zeroed, 1)
            gp.memset(xprobs[:], 0.0).then_inc(zeroed, 1)
            link(gp.memset(v_s[:], 0.0))
            gp.memset(v_s[:, :, :, :, DH:DH + 1], 1.0).then_inc(zeroed, 1)
            link(gp.memset(xv_s[:], 0.0))
            gp.memset(xv_s[:, :, :, DH:DH + 1], 1.0).then_inc(zeroed, 1)

            def leave_rest(n, use, cols):
                pool.wait_ge(misc_taken, use)
                gp.tensor_tensor(full[n][:, 0:cols], full[n][:, 0:cols], parts[n][:, 0, 0:cols],
                                 ALU.subtract).then_inc(rest_ready[n], 1)

            def low_part(n, cols, nth):
                pool.wait_ge(middle_ready[n], nth)
                gp.tensor_tensor(parts[n][:, 2, 0:cols], full[n][:, 0:cols], parts[n][:, 1, 0:cols],
                                 ALU.subtract).then_inc(low_ready[n], 1)

            leave_rest("x", 1, B * S2)
            low_part("x", B * S2, 1)

            for step in SCHEDULE:
                kind, b, k = step
                if kind == "ln_stats":
                    n = 3 * b + k
                    pool.wait_ge(var_ready, STATS[step])
                    gp.tensor_tensor(rstd[:, n], var[:, n], minus_half[:], ALU.pow).then_inc(rstd_ready, 1)
                elif kind in PROJECTED:
                    leave_rest(PROJECTED[kind], MISC0 + MISC[step], S)
                elif kind in SPLIT:
                    low_part(SPLIT[kind], S, b + (2 if kind == "split_xq" else 1))
                elif kind == "scores":
                    grp, u = k
                    pool.wait_ge(pair_taken[PAIR[step] % 2], (PAIR[step] + 1) // 2)
                    p = probs[:, grp % 2, 2 * u:2 * u + 2, :]
                    if u < 2:
                        v, pattern = p[:, :, 0:128], [[0, 2], [1, 128]]
                    elif u < 4:
                        v, pattern = p[:, :, 0:256], [[0, 2], [0, 2], [1, 128]]
                    else:
                        v, pattern = p.rearrange("p b (c q) -> p (b c) q", q=256)[:, :, 0:128], [[0, 4], [1, 128]]
                    gp.affine_select(out=v, in_=v, compare_op=ALU.is_ge, fill=0.0, base=0, pattern=pattern,
                                     channel_multiplier=-1).then_inc(causal_done, 1)
                elif kind == "expert":
                    pool.wait_ge(pair_taken[PAIR[step] % 2], (PAIR[step] + 1) // 2)
                    if T * b + k:
                        pool.wait_ge(y_summed, T * b + k)
                    y = yw[:, k % 2]
                    link(gp.tensor_tensor(y4[:], y[:, 0:4], y[:, 4:8], ALU.add))
                    link(gp.tensor_tensor(y2[:], y4[:, 0:2], y4[:, 2:4], ALU.add))
                    link(gp.tensor_tensor(y1[:], y2[:, 0], y2[:, 1], ALU.add))
                    gp.tensor_tensor(state[:, b, k], y1[:], state[:, b, k], ALU.add).then_inc(y_summed, 1)

        @block.scalar
        def _(act):
            ac = nc.scalar

            act.wait_ge(misc_full, 1)
            act.wait_ge(mask_split, 2)
            ac.copy(parts["x"][:, 0, 0:B * S2], full["x"][:, 0:B * S2]).then_inc(misc_taken, 1)
            act.wait_ge(rest_ready["x"], 1)
            ac.copy(parts["x"][:, 1, 0:B * S2], full["x"][:, 0:B * S2]).then_inc(middle_ready["x"], 1)
            act.wait_ge(zeroed, N_ZEROED)
            for b in range(B):
                act.wait_ge(misc_full, 2 + b)
                ac.copy(xv_s[0:S2, b, :, 0:DH], misc_ps[0:S2, 0:D].rearrange("p (h d) -> p h d", h=H)
                        ).then_inc(misc_taken, 1)

            for step in SCHEDULE:
                kind, b, k = step
                if kind in MISC_OF_ACT:
                    act.wait_ge(misc_full, MISC0 + MISC[step])
                if kind == "turn_x":
                    ac.copy(normed_t[k][:], misc_ps[:]).then_inc(misc_taken, 1)
                elif kind in PROJECTED:
                    n = PROJECTED[kind]
                    if n == "x":
                        if b == 0:
                            act.wait_ge(xk_stacked, 16 * STACK_DMAS)
                        else:
                            act.wait_ge(stacked["x"][(b - 1) % 2], 16 * STACK_DMAS * ((b + 1) // 2))
                    elif b:
                        act.wait_ge(stacked[n][(b - 1) % 2], 16 * STACK_DMAS * ((b + 1) // 2))
                    if n == "x":
                        ac.copy(parts[n][:, 0], misc_ps[:])
                        ac.copy(full[n][:], misc_ps[:]).then_inc(misc_taken, 1)
                    else:
                        bias = (bq_s if n == "q" else bk_s)[:, 0:1]
                        ac.activation(parts[n][:, 0], misc_ps[:], ACT.Identity, bias=bias)
                        ac.activation(full[n][:], misc_ps[:], ACT.Identity, bias=bias).then_inc(misc_taken, 1)
                elif kind in SPLIT:
                    n = SPLIT[kind]
                    act.wait_ge(rest_ready[n], b + (2 if n == "x" else 1))
                    ac.copy(parts[n][:, 1], full[n][:]).then_inc(middle_ready[n], 1)
                elif kind == "turn_peaks":
                    if b:
                        act.wait_ge(max_stacked[k], 32 * b)
                    ac.copy(peaks_t[:, k], misc_ps[0:24, 0:256].bitcast(BF16)).then_inc(misc_taken, 1)
                elif kind == "turn_xpeaks":
                    if b:
                        act.wait_ge(xmax_stacked, 32 * b)
                    ac.copy(xpeaks_t[:], misc_ps[0:48, 0:256].bitcast(BF16)).then_inc(misc_taken, 1)
                elif kind == "scores":
                    grp, u = k
                    act.wait_ge(pair_full, PAIR[step])
                    n = 4 * b + grp
                    if n >= 2:
                        act.wait_ge(values_done, 3 * (n - 1))
                        act.wait_ge(causal_done, 5 * (n - 1))
                    ac.activation(probs[:, grp % 2, 2 * u:2 * u + 2, :], pair_tile(step), ACT.Exp,
                                  scale=SCALE).then_inc(pair_taken[PAIR[step] % 2], 1)
                elif kind == "xscores":
                    act.wait_ge(pair_full, PAIR[step])
                    n = 4 * b + k // 2
                    if n >= 1:
                        act.wait_ge(misc_full, MISC0 + MISC[("xvalues", *divmod(n - 1, 4))])
                    ac.activation(xprobs[0:S2, 2 * (k % 2):2 * (k % 2) + 2, :],
                                  pair_tile(step)[0:S2], ACT.Exp, scale=SCALE
                                  ).then_inc(pair_taken[PAIR[step] % 2], 1)
                elif kind == "take_mix":
                    act.wait_ge(values_done, 3 * (4 * b + k + 1))
                    if k or b:
                        act.wait_ge(misc_full, MISC0 + MISC[("mix", b, k - 1) if k else ("mix", b - 1, 3)])
                    ac.copy(mix_t[:, 0], mix_ps[:]).then_inc(mix_taken, 1)
                elif kind == "xvalues":
                    ac.copy(mix_t[:, 1], misc_ps[:]).then_inc(misc_taken, 1)
                elif kind == "turn_mix":
                    ac.copy(mixed_t[:, k], misc_ps[:]).then_inc(misc_taken, 1)
                elif kind == "choose":
                    act.wait_ge(shifted_ready, b + 1)
                    ac.activation(g["exp"][:], g["shifted"][:], ACT.Exp).then_inc(exp_ready, 1)
                elif kind == "turn_gate":
                    ac.copy(comb_t[:], misc_ps[0:T * E, 0:128]).then_inc(misc_taken, 1)

        @block.vector
        def _(dve):
            ve = nc.vector
            chain = [0]

            def link(ins):
                chain[0] += 1
                ins.then_inc(dve_chain, 1)
                dve.wait_ge(dve_chain, chain[0])

            dve.wait_ge(weights_loaded, 16 * N_WEIGHTS)
            ve.tensor_scalar(keep[:], mask_s[:], -1.0, 1.0, ALU.mult, ALU.add)
            link(ve.tensor_scalar(neg[:], mask_s[:], MASKED, None, ALU.mult))
            for i in range(2):
                link(ve.tensor_copy(neg_parts[:, i], neg[:]))
                link(ve.tensor_tensor(neg[:], neg[:], neg_parts[:, i], ALU.subtract))
            ve.tensor_copy(neg_parts[:, 2], neg[:]).then_inc(mask_split, 1)
            ve.memset(mix_ps[:], 0.0).then_inc(mix_cleared, 1)
            dve.wait_ge(misc_full, 1)
            dve.wait_ge(mask_split, 1)
            ve.tensor_tensor(full["x"][:, 0:B * S2], misc_ps[:, 0:B * S2], keep[:], ALU.mult).then_inc(mask_split, 1)
            dve.wait_ge(zeroed, N_ZEROED)

            for step in SCHEDULE:
                kind, b, k = step
                if kind in MISC_OF_DVE:
                    dve.wait_ge(misc_full, MISC0 + MISC[step])
                if kind == "ln_stats":
                    n = 3 * b + k
                    if k == 0:
                        dve.wait_ge(x_loaded[b], 16)
                    for t in range(T):
                        last = ve.bn_stats(stats[:, n, t], state[:, b, t])
                    link(last)
                    for t in range(T):
                        last = ve.bn_aggr(moments[:, n, t], stats[:, n, t])
                    link(last)
                    ve.tensor_scalar(var[:, n], moments[:, n, :, 1], LN_EPS, None, ALU.add).then_inc(var_ready, 1)
                elif kind == "ln_norm":
                    n = 3 * b + k
                    i = NORM[step]
                    dve.wait_ge(rstd_ready, STATS[("ln_stats", b, k)])
                    if i > 2:
                        dve.wait_ge(misc_full, MISC0 + MISC[("turn_x", *NORMS[i - 3][1:])])
                    for t in range(T):
                        last = ve.tensor_scalar(normed[:, i % 2, t], state[:, b, t], moments[:, n, t, 0:1],
                                                rstd[:, n, t:t + 1], ALU.subtract, ALU.mult)
                    last.then_inc(norm_ready, 1)
                elif kind == "project_v":
                    if b >= 2:
                        dve.wait_ge(values_done, 12 * (b - 1))
                    ve.tensor_tensor(v_s[:, b % 2, :, :, 0:DH], misc_ps[:].rearrange("p (t h d) -> p t h d", t=T, h=H),
                                     bv_s[:].rearrange("p (h d) -> p h d", h=H).unsqueeze(1).broadcast_to([128, T, H, DH]),
                                     ALU.add).then_inc(misc_taken, 1)
                elif kind == "peak":
                    f, u = k
                    t, heads = PEAKS[u]
                    width = 128 * (t + 1)
                    n = sum(1 if s is not None else 2 for _, s in heads)
                    p0, s0 = heads[0]
                    dst = peaks[:, f, t].rearrange("p a s -> p (a s)")[:, 2 * p0 + (s0 or 0):2 * p0 + (s0 or 0) + n]
                    dve.wait_ge(peak_full, PEAK[step])
                    ve.tensor_reduce(dst, peak_bank(step)[:, 0:n * width].rearrange("p (h k) -> p h k", h=n),
                                     X_AXIS, ALU.max, negate=True).then_inc(peak_taken, 1)
                elif kind == "xpeak":
                    t, h, n = XPEAKS[k]
                    dve.wait_ge(peak_full, PEAK[step])
                    ve.tensor_reduce(xpeaks[:, t].rearrange("p a s -> p (a s)")[:, h:h + n],
                                     peak_bank(step)[:, 0:n * S2].rearrange("p (h k) -> p h k", h=n),
                                     X_AXIS, ALU.max, negate=True).then_inc(peak_taken, 1)
                elif kind in ("split_peaks", "split_xpeaks"):
                    if kind == "split_peaks":
                        src, left, dst, done = peaks[:, k], peak_rest[:, k], peak_parts[:, k], peaks_split
                        last_peak = ("peak", b, (k, len(PEAKS) - 1))
                        prior = ("turn_peaks", b - 1, k)
                    else:
                        src, left, dst, done = xpeaks[:], xpeak_rest[:], xpeak_parts[:], xpeaks_split
                        last_peak = ("xpeak", b, len(XPEAKS) - 1)
                        prior = ("turn_xpeaks", b - 1, k)
                    part = [dst[:, :, :, i, :].rearrange("p t s a -> p t a s") for i in range(3)]
                    dve.wait_ge(peak_taken, PEAK[last_peak])
                    if b:
                        dve.wait_ge(misc_full, MISC0 + MISC[prior])
                    link(ve.tensor_copy(part[0], src))
                    link(ve.tensor_tensor(left, src, part[0], ALU.subtract))
                    link(ve.tensor_copy(part[1], left))
                    ve.tensor_tensor(part[2], left, part[1], ALU.subtract).then_inc(done, 1)
                elif kind in ("mix", "xmix"):
                    i = int(kind == "xmix")
                    ps = misc_ps[:].rearrange("p (t j c) -> p t j c", t=T, j=4)
                    if k == 0 and b:
                        dve.wait_ge(misc_full, MISC0 + MISC[("turn_mix", b - 1, i)])
                    link(ve.reciprocal(share[:, i], ps[:, :, :, DH]))
                    ve.tensor_tensor(mixed[:, i, :, 32 * k:32 * k + 32].rearrange("p t (j d) -> p t j d", j=4),
                                     ps[:, :, :, 0:DH], share[:, i].unsqueeze(3).broadcast_to([128, T, 4, DH]),
                                     ALU.mult).then_inc(misc_taken, 1)
                elif kind == "add_attention":
                    st = state[:, b].rearrange("p t d -> p (t d)")
                    if k == 0:
                        link(ve.tensor_tensor(state[:, b], state[:, b], bp_s[:].unsqueeze(1).broadcast_to([128, T, D]),
                                              ALU.add))
                    ve.tensor_tensor(st, misc_ps[:], st, ALU.add).then_inc(misc_taken, 1)
                    dve.wait_ge(misc_taken, MISC0 + MISC[step])
                elif kind == "expert_bias":
                    st = state[:, b].rearrange("p t d -> p (t d)")
                    ve.tensor_tensor(st, misc_ps[:], st, ALU.add).then_inc(misc_taken, 1)
                elif kind == "gate":
                    link(ve.tensor_tensor(g["scores"][:], misc_ps[:, 0:T * E].rearrange("p (t e) -> p t e", t=T),
                                          gate_b_s[:].unsqueeze(1).broadcast_to([128, T, E]), ALU.add))
                    ve.tensor_scalar(g["scores"][:], g["scores"][:], FLOOR, None, ALU.max).then_inc(misc_taken, 1)
                    dve.wait_ge(misc_taken, MISC0 + MISC[step])
                    link(ve.tensor_reduce(g1["max"][:], g["scores"][:], X_AXIS, ALU.max))
                    ve.tensor_tensor(g["shifted"][:], g["scores"][:], wide(g1["max"]), ALU.subtract
                                     ).then_inc(shifted_ready, 1)
                elif kind == "choose":
                    dve.wait_ge(exp_ready, b + 1)
                    if b:
                        dve.wait_ge(misc_full, MISC0 + MISC[("turn_gate", b - 1, 0)])
                    link(ve.tensor_reduce(g1["sum"][:], g["exp"][:], X_AXIS, ALU.add))
                    link(ve.reciprocal(g1["inv"][:], g1["sum"][:]))
                    link(ve.tensor_tensor(g["p"][:], g["exp"][:], wide(g1["inv"]), ALU.mult))
                    for p, top, tied, ranked, best, one in (
                            ("p", "top", "tied", "ranked", "best", "first"),
                            ("left", "top2", "tied2", "ranked2", "best2", "second")):
                        link(ve.tensor_reduce(g1[top][:], g[p][:], X_AXIS, ALU.max))
                        link(ve.tensor_tensor(g[tied][:], g[p][:], wide(g1[top]), ALU.is_ge))
                        link(ve.tensor_tensor(g[ranked][:], g[tied][:], rank[:], ALU.mult))
                        link(ve.tensor_reduce(g1[best][:], g[ranked][:], X_AXIS, ALU.max))
                        link(ve.tensor_tensor(g[one][:], g[ranked][:], wide(g1[best]), ALU.is_ge))
                        if p == "p":
                            link(ve.scalar_tensor_tensor(out=g["left"][:], in0=g["first"][:], scalar=-4.0,
                                                         in1=g["p"][:], op0=ALU.mult, op1=ALU.add))
                    link(ve.tensor_tensor(g["chosen"][:], g["first"][:], g["second"][:], ALU.add))
                    link(ve.tensor_scalar(g["floored"][:], g["p"][:], LEAST_WEIGHT, None, ALU.max))
                    link(ve.tensor_tensor(g["kept"][:], g["floored"][:], g["chosen"][:], ALU.mult))
                    link(ve.tensor_reduce(g1["total"][:], g["kept"][:], X_AXIS, ALU.add))
                    link(ve.reciprocal(g1["inv_total"][:], g1["total"][:]))
                    ve.scalar_tensor_tensor(out=g["comb"][:], in0=g["kept"][:], scalar=1.0 / TOP_K,
                                            in1=wide(g1["inv_total"]), op0=ALU.mult, op1=ALU.mult
                                            ).then_inc(comb_ready, 1)
                    dve.wait_ge(comb_ready, b + 1)
                elif kind == "expert":
                    dve.wait_ge(pair_full, PAIR[step])
                    n = T * b + k
                    if n >= 2:
                        dve.wait_ge(y_summed, n - 1)
                    ve.tensor_tensor(yw[:, k % 2], pair_tile(step).rearrange("p b (e d) -> p (b e) d", d=D),
                                     g["comb"][:, k].unsqueeze(2).broadcast_to([128, E, D]), ALU.mult
                                     ).then_inc(pair_taken[PAIR[step] % 2], 1)

        @block.tensor
        def _(pe):
            te = nc.tensor

            def misc_free(use):
                if use > 1:
                    pe.wait_ge(misc_taken, use - 1)

            def pair_free(step):
                n = PAIR[step]
                if n > 2:
                    pe.wait_ge(pair_taken[n % 2], (n - 1) // 2)

            def peak_free(step):
                if PEAK[step] > 2:
                    pe.wait_ge(peak_taken, PEAK[step] - 2)

            def product(weight, moving, use, tiles=False):
                misc_free(use)
                if not tiles:
                    last = te.matmul(misc_ps[:], weight[:], moving, start=True, stop=True)
                else:
                    cols = weight.shape[-1]
                    for t in range(T):
                        last = te.matmul(misc_ps[:, cols * t:cols * t + cols], moving[:, 128 * t:128 * t + 128],
                                         weight[:], start=True, stop=True)
                last.then_inc(misc_full, 1)

            pe.wait_ge(weights_loaded, 16 * N_WEIGHTS)
            te.matmul(misc_ps[:, 0:B * S2], xwk_s[:], ctx_s[:], start=True, stop=True).then_inc(misc_full, 1)
            for b in range(B):
                misc_free(2 + b)
                te.matmul(misc_ps[0:S2, 0:D], ctx_s[:, S2 * b:S2 * b + S2], xwv_s[:], start=True, stop=True
                          ).then_inc(misc_full, 1)
            pe.wait_ge(zeroed, N_ZEROED)
            pe.wait_ge(ones_stacked, 16 * N_ONES)
            pe.wait_ge(mix_cleared, 1)

            for step in SCHEDULE:
                kind, b, k = step
                use = MISC0 + MISC.get(step, 0)
                if kind == "turn_x":
                    i = NORM[("ln_norm", b, k)]
                    pe.wait_ge(norm_ready, i)
                    misc_free(use)
                    for t in range(T):
                        last = te.transpose(misc_ps[:, 128 * t:128 * t + 128], normed[:, i % 2, t], ident[:])
                    last.then_inc(misc_full, 1)
                elif kind == "project_q":
                    product(wq_s, normed_t[0][:], use)
                elif kind == "project_k":
                    product(wk_s, normed_t[0][:], use)
                elif kind == "project_v":
                    product(wv_s, normed_t[0], use, tiles=True)
                elif kind == "project_xq":
                    product(xwq_s, normed_t[1][:], use)
                elif kind == "gate":
                    product(gate_w_s, normed_t[2], use, tiles=True)
                elif kind == "peak":
                    f, u = k
                    t, heads = PEAKS[u]
                    width = 128 * (t + 1)
                    if u == 0:
                        pe.wait_ge(stacked["q"][b % 2], 16 * STACK_DMAS * (b // 2 + 1))
                        pe.wait_ge(stacked["k"][b % 2], 16 * STACK_DMAS * (b // 2 + 1))
                    peak_free(step)
                    bank = peak_bank(step)
                    n = sum(1 if s is not None else 2 for _, s in heads)
                    diagonal = bank[:, 0:n * width].rearrange("p (h k) -> p h k", h=n)[:, :, width - 128:width]
                    te.matmul(diagonal, ident_b[:], causal[:, 0:n], start=True, stop=False, skip_group_check=True)
                    for i, (p, s) in enumerate(heads):
                        q = q_stack[0:MAX_ROW, b % 2, 4 * f + p, 128 * t:128 * t + 128]
                        if s is None:
                            keys = k_stack[0:MAX_ROW, b % 2, :, 4 * f + p, 0:width]
                            dst = bank[:, 2 * width * i:2 * width * (i + 1)].rearrange("p (s k) -> p s k", s=2)
                        else:
                            keys = k_stack[0:MAX_ROW, b % 2, s, 4 * f + p, 0:width]
                            dst = bank[:, 0:width]
                        last = te.matmul(dst, q, keys, start=False, stop=(i == len(heads) - 1), skip_group_check=True)
                    last.then_inc(peak_full, 1)
                elif kind == "xpeak":
                    t, h, n = XPEAKS[k]
                    if k == 0:
                        pe.wait_ge(stacked["x"][b % 2], 16 * STACK_DMAS * (b // 2 + 1))
                        pe.wait_ge(xk_stacked, 16 * STACK_DMAS)
                        pe.wait_ge(masks_stacked, 16 * H)
                    peak_free(step)
                    for i in range(n):
                        p, s = (h + i) // 2, (h + i) % 2
                        last = te.matmul(peak_bank(step)[:, S2 * i:S2 * i + S2],
                                         xq_stack[0:MAX_ROW, p, 128 * t:128 * t + 128],
                                         xk_stack[0:MAX_ROW, s, p, S2 * b:S2 * b + S2], start=True, stop=True)
                    last.then_inc(peak_full, 1)
                elif kind in ("turn_peaks", "turn_xpeaks"):
                    self_attention = kind == "turn_peaks"
                    src = peak_parts[:, k] if self_attention else xpeak_parts[:]
                    rows = 24 if self_attention else 48
                    pe.wait_ge(peaks_split if self_attention else xpeaks_split, 2 * b + k + 1 if self_attention else b + 1)
                    misc_free(use)
                    for t in range(T):
                        last = te.transpose(misc_ps[0:rows, 64 * t:64 * t + 64].bitcast(BF16),
                                            src[:, t].rearrange("p s i a -> p (s i a)"), ident_b[:])
                    last.then_inc(misc_full, 1)
                elif kind == "scores":
                    grp, u = k
                    if u == 0 and grp % 2 == 0:
                        pe.wait_ge(max_stacked[grp // 2], 32 * (b + 1))
                    pair_free(step)
                    tile = pair_tile(step)
                    for bank, col, j, kt in SCORES[u]:
                        h = 4 * grp + j
                        p, s = h // 2, h % 2
                        n = S - 128 * kt
                        last = te.matmul(tile[:, bank, col:col + n], k_stack[:, b % 2, s, p, 128 * kt:128 * kt + 128],
                                         q_stack[:, b % 2, p, 128 * kt:S], start=True, stop=True)
                    last.then_inc(pair_full, 1)
                elif kind == "values":
                    grp, v = k
                    tiles, u = VALUES[v]
                    pe.wait_ge(causal_done, 5 * (4 * b + grp) + u + 1)
                    if v == 0:
                        if MIX[("take_mix", b, grp)] > 1:
                            pe.wait_ge(mix_taken, MIX[("take_mix", b, grp)] - 1)
                        pe.wait_ge(misc_taken, MISC0 + MISC[("project_v", b, 0)])
                    for kt in tiles:
                        for j in range(4):
                            bank, col = PLACE[(kt, j)]
                            last = te.matmul(mix_ps[32 * j:32 * j + VW, 128 * kt:S], v_s[:, b % 2, kt, 4 * grp + j],
                                             probs[:, grp % 2, bank, col:col + S - 128 * kt],
                                             start=(kt == 0), stop=(kt == 2), skip_group_check=True)
                    last.then_inc(values_done, 1)
                elif kind == "xscores":
                    if k == 0:
                        pe.wait_ge(xmax_stacked, 32 * (b + 1))
                    pair_free(step)
                    for s in range(2):
                        last = te.matmul(pair_tile(step)[0:S2, s], xk_stack[:, s, k, S2 * b:S2 * b + S2],
                                         xq_stack[:, k], start=True, stop=True)
                    last.then_inc(pair_full, 1)
                elif kind == "xvalues":
                    second = PAIR[("xscores", b, 2 * k + 1)]
                    first = PAIR[("xscores", b, 2 * k)]
                    for n in (first, second):
                        pe.wait_ge(pair_taken[n % 2], (n + 1) // 2)
                    misc_free(use)
                    for j in range(4):
                        last = te.matmul(misc_ps[32 * j:32 * j + VW, :], xv_s[:, b, 4 * k + j],
                                         xprobs[:, j], start=True, stop=True)
                    last.then_inc(misc_full, 1)
                elif kind in ("mix", "xmix"):
                    i = int(kind == "xmix")
                    if i:
                        pe.wait_ge(misc_taken, MISC0 + MISC[("xvalues", b, k)])
                    else:
                        pe.wait_ge(mix_taken, MIX[("take_mix", b, k)])
                    misc_free(use)
                    for t in range(T):
                        last = te.transpose(misc_ps[:, 128 * t:128 * t + 128], mix_t[:, i, 128 * t:128 * t + 128],
                                            ident[:])
                    last.then_inc(misc_full, 1)
                elif kind == "turn_mix":
                    pe.wait_ge(misc_taken, MISC0 + MISC[("xmix" if k else "mix", b, 3)])
                    misc_free(use)
                    for t in range(T):
                        last = te.transpose(misc_ps[:, 128 * t:128 * t + 128], mixed[:, k, t], ident[:])
                    last.then_inc(misc_full, 1)
                elif kind == "add_attention":
                    product(xwo_s if k else wp_s, mixed_t[:, k], use, tiles=True)
                elif kind == "turn_gate":
                    pe.wait_ge(comb_ready, b + 1)
                    misc_free(use)
                    te.transpose(misc_ps[0:T * E, 0:128], g["comb"][:].rearrange("p t e -> p (t e)"), ident[:]
                                 ).then_inc(misc_full, 1)
                elif kind == "expert_bias":
                    misc_free(use)
                    for t in range(T):
                        last = te.matmul(misc_ps[:, D * t:D * t + D], comb_t[:], expert_b_s[:, t], start=True, stop=True)
                    last.then_inc(misc_full, 1)
                elif kind == "expert":
                    pair_free(step)
                    for n in range(2):
                        last = te.matmul(pair_tile(step)[:, n], normed_t[2][:, 128 * k:128 * k + 128],
                                         expert_w_s[:, 4 * n:4 * n + 4].rearrange("d e f -> d (e f)"),
                                         start=True, stop=True)
                    last.then_inc(pair_full, 1)


def kernel(**inputs):
    import concourse.bacc as bacc
    from concourse.bass_utils import run_bass_kernel_spmd

    a = {k: np.asarray(v) for k, v in inputs.items()}

    def by_slot(w):
        return w.reshape(*w.shape[:-1], PAIRS, 2, DH).swapaxes(-3, -2).swapaxes(-2, -1).reshape(w.shape)

    arrays = {
        "x": a["x"],
        "ctx_t": a["ctx_1024"].transpose(2, 0, 1).reshape(D, B * S2),
        "mask": a["mask_Bx1x1xS2_bk0"].reshape(B * S2),
        "wq": by_slot(a["L0_attn_Wq"]), "bq": by_slot(a["L0_attn_bq"]).reshape(D, 1),
        "wk": by_slot(a["L0_attn_Wk"]), "bk": by_slot(a["L0_attn_bk"]).reshape(D, 1),
        "wv": a["L0_attn_Wv"], "bv": a["L0_attn_bv"],
        "wp": a["L0_attn_Wp"], "bp": a["L0_attn_bp"],
        "xwq": by_slot(a["L0_xattn_Wq"].T), "xwk": by_slot(a["L0_xattn_Wk"].T),
        "xwv": a["L0_xattn_Wv"].T, "xwo": a["L0_xattn_Wo"].T,
        "gate_w": a["L0_ffn_gate_W"], "gate_b": a["L0_ffn_gate_b"],
        "expert_w": a["L0_ffn_expert_W"], "expert_b": a["L0_ffn_expert_b"],
    }
    arrays = {k: np.ascontiguousarray(v) for k, v in arrays.items()}
    nc = bacc.Bacc("TRN2", target_bir_lowering=False, num_devices=1)
    args = [nc.dram_tensor(f"in_{k}", v.shape, mybir.dt.from_np(v.dtype), kind="ExternalInput").ap()
            for k, v in arrays.items()]
    out = nc.dram_tensor("out", (B, S, D), F32, kind="ExternalOutput").ap()
    names = list(arrays)
    decoder_layer(nc, **dict(zip(names, args)), out=out)
    r = run_bass_kernel_spmd(nc, [{f"in_{k}": v for k, v in arrays.items()}], core_ids=[0])
    return r.results[0]["out"]
```

```python
from contextlib import ExitStack

import numpy as np

import concourse.bass as bass
from concourse import mybir

F32 = mybir.dt.float32
BF16 = mybir.dt.bfloat16
U8 = mybir.dt.uint8
ALU = mybir.AluOpType
ACT = mybir.ActivationFunctionType
X_AXIS = mybir.AxisListType.X

B, S, D, H, E = 4, 512, 128, 16, 8
DH = D // H
S2 = 77
T = S // 128
PAIRS = H // 2
SCALE = float(1.0 / np.sqrt(np.float32(DH)))
MASKED = -1.0e9
FUTURE = -3.0e38
FLOOR, LEAST_WEIGHT, TOP_K = 1e-4, 0.1, 2
LN_EPS = 1e-5
VW = DH + 1

SLOT_ROWS = 6 * DH
MASK_ROW, MAX_ROW = 96, 122
Q_PARTS = (0, 0, 0, 1, 1, 2)
K_PARTS = (0, 1, 2, 0, 1, 0)
STACK_DMAS = 2 * len(Q_PARTS)

PEAKS = ([(0, [(p, None) for p in (2 * i, 2 * i + 1)]) for i in range(2)]
         + [(1, [(p, None)]) for p in range(4)]
         + [(t, [(p, s)]) for t in (2, 3) for p in range(4) for s in range(2)])
XPEAKS = [(t, h, n) for t in range(T) for h, n in ((0, 6), (6, 5), (11, 5))]
SCORES = ([[(0, j, 0)] for j in range(4)]
          + [[(0, j, 3), (128, j, 1)] for j in range(4)]
          + [[(0, j, 2), (256, j + 1, 2)] for j in (0, 2)])
PLACE = {(kt, j): (u, col) for u, unit in enumerate(SCORES) for col, j, kt in unit}
VALUES = [((0,), 1), ((1, 3), 3), ((2,), 4)]


XPROBS = 6
UNITS = 3

TAKES = {"turn_x": 1.2, "ln_stats": 2.5, "ln_norm": 1.2, "project_q": 2, "project_k": 2, "split_q": 2,
         "project_v": 1, "split_k": 8, "turn_mix": 1.2, "add_attention": 1.8, "project_xq": 2.2, "split_xq": 11,
         "split_xpeaks": 1, "turn_xpeaks": 5, "xvalues": 1.2, "xmix": 1.2, "gate": 1, "choose": 4.5,
         "turn_gate": 1, "expert_bias": 1, "split_peaks": 1, "context_keys": 3, "split_context": 3}


def spread(items, lo, hi):
    takes = [TAKES.get(kind, 0.6) for kind, _, _ in items]
    return [(lo + (hi - lo) * (sum(takes[:i]) + 0.3) / sum(takes), x) for i, x in enumerate(items)]


def middle(items):
    takes = [TAKES.get(kind, 0.6) for kind, _, _ in items]
    return next(i for i in range(len(items)) if 2 * sum(takes[:i]) >= sum(takes))


def plan():
    def norm(b, n):
        return [("ln_stats", b, n), ("ln_norm", b, n), ("turn_x", b, n)]

    def prepare(b):
        return norm(b, 0) + [("project_q", b, 0), ("project_k", b, 0), ("split_q", b, 0), ("project_v", b, 0),
                             ("split_k", b, 0)]

    def peaks(b, f):
        return [("peak", b, (f, u)) for u in range(len(PEAKS))] + [("split_peaks", b, f), ("turn_peaks", b, f)]

    def attend(b, f):
        out, late = [], []
        for g in (2 * f, 2 * f + 1):
            s = [("scores", b, (g, u)) for u in range(len(SCORES))]
            v = [("values", b, (g, v)) for v in range(3)]
            out += s[0:3] + late + s[3:6] + [v[0]] + s[6:] + [v[1]]
            late = [v[2], ("take_mix", b, g), ("mix", b, g)]
        out += late
        return out

    def cross(b):
        out = [("turn_mix", b, 0), ("add_attention", b, 0)] + norm(b, 1) + [("project_xq", b, 0), ("split_xq", b, 0)]
        out += [("xpeak", b, u) for u in range(len(XPEAKS))] + [("split_xpeaks", b, 0), ("turn_xpeaks", b, 0)]
        for g in range(4):
            out += [("xscores", b, h) for h in range(4 * g + 2 * (g > 0), min(4 * g + 6, H))]
            out += [("xvalues", b, g), ("xmix", b, g)]
        return out + [("turn_mix", b, 1), ("add_attention", b, 1)]

    def experts(b):
        out = norm(b, 2) + [("gate", b, 0), ("choose", b, 0)] + [("expert", b, u) for u in range(UNITS)]
        out += [("turn_gate", b, 0), ("expert_bias", b, 0)]
        return out + [("expert", b, u) for u in range(UNITS, 2 * T)] + [("store", b, 0)]

    context = [("context_keys", 0, 0), ("split_context", 0, 0)] + [("context_values", b, 0) for b in range(B)]
    steps = prepare(0) + peaks(0, 0)
    for b in range(B):
        tail = cross(b - 1) if b else []
        if 0 < b < B - 1:
            tail += experts(b - 1)
        half = middle(tail) if tail else 0
        first = spread(attend(b, 0), 0, 1) + spread(peaks(b, 1), 0, 0.8)
        second = spread(attend(b, 1), 0, 1)
        if b + 1 < B:
            first += spread(prepare(b + 1), 0, 0.8)
            second += spread(peaks(b + 1, 0), 0, 0.8)
        if b == 0:
            first += spread(context, 0.5, 1)
        if tail:
            first += spread(tail[:half], 0, 1)
            second += spread(tail[half:], 0, 1)
        for part in (first, second):
            steps += [x for _, x in sorted(part, key=lambda y: y[0])]
    last = cross(B - 1)
    gap = last.index(("split_xq", B - 1, 0)) + 1
    return steps + last[:gap] + experts(B - 2) + last[gap:] + experts(B - 1)


SCHEDULE = plan()


def uses(*kinds):
    return {x: n + 1 for n, x in enumerate(x for x in SCHEDULE if x[0] in kinds)}


MISC = uses("context_keys", "context_values", "turn_x", "project_q", "project_k", "project_v", "turn_peaks", "mix", "turn_mix",
            "add_attention", "project_xq", "turn_xpeaks", "xvalues", "xmix", "gate", "turn_gate", "expert_bias")
UNIT = uses("scores", "xscores", "expert")
PEAK = uses("peak", "xpeak")
MIX = uses("take_mix")
STATS = uses("ln_stats")
NORM = uses("ln_norm")
NORMS = list(NORM)
MISC_OF_ACT = ("turn_x", "project_q", "project_k", "project_xq", "turn_peaks", "turn_xpeaks", "turn_mix",
               "turn_gate", "xvalues", "context_values")
MISC_OF_DVE = ("context_keys", "project_v", "mix", "xmix", "add_attention", "gate", "expert_bias")


def decoder_layer(nc, x, ctx_t, mask, wq, bq, wk, bk, wv, bv, wp, bp, xwq, xwk, xwv, xwo,
                  gate_w, gate_b, expert_w, expert_b, out):
    with ExitStack() as stack:
        def sb(name, shape, dt=F32):
            return stack.enter_context(nc.sbuf_tensor(name, shape, dt))

        def psum(name, shape):
            return stack.enter_context(nc.psum_tensor(name, shape, F32))

        def sem(name):
            return stack.enter_context(nc.semaphore(name))

        peak_ps = psum("peak_ps", [128, 2, 512])
        unit_ps = psum("unit_ps", [128, UNITS, 512])
        mix_ps = psum("mix_ps", [128, 512])
        misc_banks = psum("misc_banks", [128, 2, 512])

        wq_s, wk_s, wv_s, wp_s, xwq_s, xwk_s, xwv_s, xwo_s = (
            sb(n, [D, D]) for n in ("wq_s", "wk_s", "wv_s", "wp_s", "xwq_s", "xwk_s", "xwv_s", "xwo_s"))
        bq_s, bk_s = sb("bq_s", [D, 1]), sb("bk_s", [D, 1])
        bv_s, bp_s = sb("bv_s", [128, D]), sb("bp_s", [128, D])
        gate_w_s, gate_b_s = sb("gate_w_s", [D, E]), sb("gate_b_s", [128, E])
        expert_w_s = sb("expert_w_s", [D, E, D])
        expert_b_s = sb("expert_b_s", [T * E, T, D])
        ctx_s = sb("ctx_s", [D, B * S2])
        mask_s = sb("mask_s", [128, B * S2], U8)
        ident = sb("ident", [128, 128])
        ident_b = sb("ident_b", [128, 128], BF16)
        causal = sb("causal", [128, 4, 128], BF16)
        ones_b = sb("ones_b", [128, 512], BF16)
        minus_half = sb("minus_half", [128, T])
        rank = sb("rank", [128, T, E])
        keep = sb("keep", [128, B * S2])
        neg = sb("neg", [128, B * S2])
        neg_parts = sb("neg_parts", [128, 3, B * S2], BF16)

        state = sb("state", [128, B, T, D])
        stats = sb("stats", [128, 3 * B, T, 6])
        moments = sb("moments", [128, 3 * B, T, 2])
        var = sb("var", [128, 3 * B, T])
        rstd = sb("rstd", [128, 3 * B, T])
        normed = sb("normed", [128, 2, T, D])
        normed_t = [sb(f"normed_t{n}", [D, S]) for n in range(3)]

        kinds = ("q", "k", "x")
        full = {n: sb(f"full_{n}", [D, S]) for n in kinds}
        parts = {n: sb(f"parts_{n}", [D, 3, S], BF16) for n in kinds}
        q_stack = sb("q_stack", [128, 2, PAIRS, S], BF16)
        k_stack = sb("k_stack", [128, 2, 2, PAIRS, S], BF16)
        xq_stack = sb("xq_stack", [128, PAIRS, S], BF16)
        xk_stack = sb("xk_stack", [128, 2, PAIRS, B * S2], BF16)
        v_s = sb("v_s", [128, 2, T, H, VW])
        xv_s = sb("xv_s", [128, B, H, VW])

        peaks = sb("peaks", [128, 2, T, 4, 2])
        peak_rest = sb("peak_rest", [128, 2, T, 4, 2])
        peak_parts = sb("peak_parts", [128, 2, T, 2, 3, 4], BF16)
        peaks_t = sb("peaks_t", [24, 2, S], BF16)
        xpeaks = sb("xpeaks", [128, T, PAIRS, 2])
        xpeak_rest = sb("xpeak_rest", [128, T, PAIRS, 2])
        xpeak_parts = sb("xpeak_parts", [128, T, 2, 3, PAIRS], BF16)
        xpeaks_t = sb("xpeaks_t", [48, S], BF16)

        probs = sb("probs", [128, 2, 10, 512])
        xprobs = sb("xprobs", [128, XPROBS, 512])
        mix_t = sb("mix_t", [128, 2, 512])
        share = sb("share", [128, 2, T, 4])
        mixed = sb("mixed", [128, 2, T, D])
        mixed_t = sb("mixed_t", [D, 2, S])

        g = {n: sb(f"g_{n}", [128, T, E]) for n in
             ("scores", "shifted", "exp", "p", "tied", "ranked", "first", "left", "tied2", "ranked2",
              "second", "chosen", "floored", "kept", "comb")}
        g1 = {n: sb(f"g1_{n}", [128, T]) for n in
              ("max", "sum", "inv", "top", "best", "top2", "best2", "total", "inv_total")}
        comb_t = sb("comb_t", [T * E, 128])
        yw = sb("yw", [128, 2, E, D])

        x_loaded = [sem(f"x_loaded{b}") for b in range(B)]
        first_loaded = sem("first_loaded")
        rest_loaded = sem("rest_loaded")
        biases_loaded = sem("biases_loaded")
        cleared = sem("cleared")
        cleared_later = sem("cleared_later")
        ones_stacked = sem("ones_stacked")
        mask_split = sem("mask_split")
        var_ready, rstd_ready, norm_ready = sem("var_ready"), sem("rstd_ready"), sem("norm_ready")
        misc_full = sem("misc_full")
        misc_taken = [sem("misc_taken0"), sem("misc_taken1")]
        unit_full = sem("unit_full")
        unit_taken = [sem(f"unit_taken{i}") for i in range(UNITS)]
        peak_full, peak_taken = sem("peak_full"), sem("peak_taken")
        mix_taken = sem("mix_taken")
        high_ready = {n: sem(f"high_ready_{n}") for n in kinds}
        rest_ready = {n: sem(f"rest_ready_{n}") for n in kinds}
        middle_ready = {n: sem(f"middle_ready_{n}") for n in kinds}
        low_ready = {n: sem(f"low_ready_{n}") for n in kinds}
        stacked = {n: [sem(f"stacked_{n}{i}") for i in range(2)] for n in kinds}
        xk_stacked = sem("xk_stacked")
        peaks_split, xpeaks_split = sem("peaks_split"), sem("xpeaks_split")
        max_stacked = [sem("max_stacked0"), sem("max_stacked1")]
        xmax_stacked = sem("xmax_stacked")
        causal_done = sem("causal_done")
        values_done = sem("values_done")
        shifted_ready, exp_ready, comb_ready = sem("shifted_ready"), sem("exp_ready"), sem("comb_ready")
        y_summed = sem("y_summed")
        stored = sem("stored")
        dve_chain, pool_chain = sem("dve_chain"), sem("pool_chain")

        block = stack.enter_context(nc.Block())

        FIRST = [(wq_s[:], wq), (bq_s[:], bq), (wk_s[:], wk), (bk_s[:], bk), (wv_s[:], wv),
                 (bv_s[:], bv.partition_broadcast(128))]
        REST = [(xwk_s[:], xwk), (ctx_s[:], ctx_t), (mask_s[:], mask.partition_broadcast(128)), (xwv_s[:], xwv),
                (wp_s[:], wp), (bp_s[:], bp.partition_broadcast(128)), (xwq_s[:], xwq), (xwo_s[:], xwo),
                (gate_w_s[:], gate_w), (gate_b_s[:], gate_b.partition_broadcast(128)),
                (expert_w_s[:], expert_w.rearrange("e d f -> d e f"))]
        N_REST = len(REST)
        CLEARED = ["ident", "minus_half", "q_stack", "k_stack", "causal", "v_s", "xk_stack", "xv_s", "expert_b_s",
                   "rank"]

        N_XK = STACK_DMAS + 3 + 6

        def wait_cleared(eng, name):
            eng.wait_ge(cleared, CLEARED.index(name) + 1)

        PROJECTED = {"project_q": "q", "project_k": "k", "project_xq": "x"}
        SPLIT = {"split_q": "q", "split_k": "k", "split_xq": "x"}

        def wide(a):
            return a[:].unsqueeze(2).broadcast_to([128, T, E])

        def wait_misc_taken(eng, use):
            eng.wait_ge(misc_taken[use % 2], (use + 1) // 2)

        def wait_unit_taken(eng, step):
            eng.wait_ge(unit_taken[UNIT[step] % UNITS], (UNIT[step] + UNITS - 1) // UNITS)

        def peak_bank(step):
            return peak_ps[:, PEAK[step] % 2, :]

        def unit_bank(step):
            return unit_ps[:, UNIT[step] % UNITS]

        @block.sync
        def _(sp):
            for b in range(B):
                sp.dma_start(state[:, b], x[b].rearrange("(t p) d -> p t d", p=128)).then_inc(x_loaded[b], 16)
                if b == 0:
                    for dst, src in FIRST:
                        sp.dma_start(dst, src).then_inc(first_loaded, 16)
            for dst, src in REST:
                sp.dma_start(dst, src).then_inc(rest_loaded, 16)
            ones = ones_b[0:3 * PAIRS, :]

            def stack_free(b):
                if b >= 2:
                    sp.wait_ge(values_done, 12 * (b - 1))

            def copy_parts(n, nth, order, rows, cols, done):
                for part, ready in enumerate((high_ready[n], middle_ready[n], low_ready[n])):
                    sp.wait_ge(ready, nth)
                    for i in range(len(order)):
                        if order[i] == part:
                            for s in range(2):
                                sp.dma_start(rows(SLOT_ROWS * s + DH * i, s),
                                             parts[n][64 * s:64 * s + 64, part, 0:cols]).then_inc(done, 16)

            for step in SCHEDULE:
                kind, b, k = step
                if kind == "peak" and (b, k) == (0, (0, 0)):
                    wait_cleared(sp, "k_stack")
                    sp.wait_ge(cleared_later, 3)
                    for i in range(2):
                        for s in range(2):
                            r = MAX_ROW + 3 * s
                            sp.dma_start(k_stack[r:r + 3, i, s], ones).then_inc(ones_stacked, 16)
                elif kind == "context_keys":
                    wait_cleared(sp, "expert_b_s")
                    sp.wait_ge(cleared_later, 4)
                    for t in range(T):
                        sp.dma_start(expert_b_s[E * t:E * t + E, t, :], expert_b).then_inc(biases_loaded, 16)
                    sp.dma_start(xq_stack[MASK_ROW:MASK_ROW + 3], ones).then_inc(xk_stacked, 16)
                    for s in range(2):
                        r = MAX_ROW + 3 * s
                        sp.dma_start(xk_stack[r:r + 3, s], ones_b[0:3 * PAIRS, 0:B * S2]).then_inc(xk_stacked, 16)
                    sp.wait_ge(mask_split, 1)
                    for s in range(2):
                        for i in range(3):
                            sp.dma_start(xk_stack[MASK_ROW + i:MASK_ROW + i + 1, s],
                                         neg_parts[0:1, i].unsqueeze(1).broadcast_to([1, PAIRS, B * S2])
                                         ).then_inc(xk_stacked, 16)
                elif kind == "split_context":
                    copy_parts("x", 1, K_PARTS, lambda r, s: xk_stack[r:r + DH, s], B * S2, xk_stacked)
                elif kind == "split_q":
                    stack_free(b)
                    copy_parts("q", b + 1, Q_PARTS, lambda r, s: q_stack[r:r + DH, b % 2], S, stacked["q"][b % 2])
                elif kind == "split_k":
                    stack_free(b)
                    copy_parts("k", b + 1, K_PARTS, lambda r, s: k_stack[r:r + DH, b % 2, s], S, stacked["k"][b % 2])
                elif kind == "split_xq":
                    if b >= 1:
                        sp.wait_ge(misc_full, MISC[("xvalues", b - 1, 3)])
                    copy_parts("x", b + 2, Q_PARTS, lambda r, s: xq_stack[r:r + DH], S, stacked["x"][b % 2])
                elif kind == "turn_peaks":
                    wait_misc_taken(sp, MISC[step])
                    for s in range(2):
                        r = MAX_ROW + 3 * s
                        sp.dma_start(q_stack[r:r + 3, b % 2, 4 * k:4 * k + 4],
                                     peaks_t[12 * s:12 * s + 12, k]).then_inc(max_stacked[k], 16)
                elif kind == "turn_xpeaks":
                    wait_misc_taken(sp, MISC[step])
                    for s in range(2):
                        r = MAX_ROW + 3 * s
                        sp.dma_start(xq_stack[r:r + 3], xpeaks_t[24 * s:24 * s + 24, :]).then_inc(xmax_stacked, 16)
                elif kind == "store":
                    sp.wait_ge(y_summed, T * (b + 1))
                    sp.dma_start(out[b].rearrange("(t p) d -> p t d", p=128), state[:, b]).then_inc(stored, 16)
            sp.wait_ge(stored, 16 * B)

        @block.gpsimd
        def _(pool):
            gp = nc.gpsimd
            chain = [0]

            def link(ins):
                chain[0] += 1
                ins.then_inc(pool_chain, 1)
                pool.wait_ge(pool_chain, chain[0])

            def clear(buffer):
                v = buffer[:] if buffer.dtype == F32 else buffer[:].bitcast(F32)
                return gp.memset(v, 0.0)

            link(gp.memset(ident[:], 0.0))
            link(gp.affine_select(out=ident[:], in_=ident[:], compare_op=ALU.not_equal, fill=1.0, base=0,
                                  pattern=[[-1, 128]], channel_multiplier=1))
            gp.tensor_copy(ident_b[:], ident[:]).then_inc(cleared, 1)
            gp.memset(minus_half[:], -0.5).then_inc(cleared, 1)
            gp.memset(ones_b[:], 1.0)
            gp.memset(q_stack[:, 0].bitcast(F32), 0.0).then_inc(cleared, 1)
            gp.memset(k_stack[:, 0].bitcast(F32), 0.0).then_inc(cleared, 1)

            def leave_rest(n, use, cols):
                wait_misc_taken(pool, use)
                gp.tensor_tensor(full[n][:, 0:cols], full[n][:, 0:cols], parts[n][:, 0, 0:cols],
                                 ALU.subtract).then_inc(rest_ready[n], 1)

            def low_part(n, cols, nth):
                pool.wait_ge(middle_ready[n], nth)
                gp.tensor_tensor(parts[n][:, 2, 0:cols], full[n][:, 0:cols], parts[n][:, 1, 0:cols],
                                 ALU.subtract).then_inc(low_ready[n], 1)

            for step in SCHEDULE:
                kind, b, k = step
                if kind == "ln_stats":
                    n = 3 * b + k
                    pool.wait_ge(var_ready, STATS[step])
                    if n == 0:
                        wait_cleared(pool, "minus_half")
                    gp.tensor_tensor(rstd[:, n], var[:, n], minus_half[:], ALU.pow).then_inc(rstd_ready, 1)
                    if n == 0:
                        link(gp.memset(causal[:], 0.0))
                        gp.affine_select(out=causal[:], in_=causal[:], compare_op=ALU.is_ge, fill=FUTURE, base=0,
                                         pattern=[[0, 4], [-1, 128]], channel_multiplier=1).then_inc(cleared, 1)
                        link(clear(v_s))
                        gp.memset(v_s[:, :, :, :, DH:DH + 1], 1.0).then_inc(cleared, 1)
                elif kind in PROJECTED:
                    leave_rest(PROJECTED[kind], MISC[step], S)
                elif kind in SPLIT:
                    low_part(SPLIT[kind], S, b + (2 if kind == "split_xq" else 1))
                    if kind == "split_k" and b == 0:
                        clear(xk_stack).then_inc(cleared, 1)
                        gp.memset(xv_s[:, :, :, DH:DH + 1], 1.0).then_inc(cleared, 1)
                        clear(expert_b_s).then_inc(cleared, 1)
                        for e in range(E):
                            last = gp.memset(rank[:, :, e:e + 1], float(E - e))
                        last.then_inc(cleared, 1)
                elif kind == "context_keys":
                    pool.wait_ge(high_ready["x"], 1)
                    gp.tensor_tensor(full["x"][:, 0:B * S2], full["x"][:, 0:B * S2], parts["x"][:, 0, 0:B * S2],
                                     ALU.subtract).then_inc(rest_ready["x"], 1)
                elif kind == "split_context":
                    low_part("x", B * S2, 1)
                elif kind == "scores":
                    grp, u = k
                    if u % 2 == 0:
                        continue
                    wait_unit_taken(pool, step)
                    p = probs[:, grp % 2, u - 1:u + 1, :]
                    if u < 4:
                        v, pattern = p[:, :, 0:128], [[0, 2], [1, 128]]
                    elif u < 8:
                        v, pattern = p[:, :, 0:256], [[0, 2], [0, 2], [1, 128]]
                    else:
                        v, pattern = p.rearrange("p b (c q) -> p (b c) q", q=256)[:, :, 0:128], [[0, 4], [1, 128]]
                    gp.affine_select(out=v, in_=v, compare_op=ALU.is_ge, fill=0.0, base=0, pattern=pattern,
                                     channel_multiplier=-1).then_inc(causal_done, 1)
                elif kind == "expert" and k % 2:
                    wait_unit_taken(pool, step)
                    t = k // 2
                    if T * b + t:
                        pool.wait_ge(y_summed, T * b + t)
                    y = yw[:, t % 2]
                    for n in (4, 2, 1):
                        link(gp.tensor_tensor(y[:, 0:n], y[:, 0:n], y[:, n:2 * n], ALU.add))
                    if t == 0:
                        wait_misc_taken(pool, MISC[("expert_bias", b, 0)])
                    gp.tensor_tensor(state[:, b, t], y[:, 0], state[:, b, t], ALU.add).then_inc(y_summed, 1)

        @block.scalar
        def _(act):
            ac = nc.scalar

            for step in SCHEDULE:
                kind, b, k = step
                if kind in MISC_OF_ACT:
                    act.wait_ge(misc_full, MISC[step])
                    misc, taken = misc_banks[:, MISC[step] % 2], misc_taken[MISC[step] % 2]
                if kind == "context_keys":
                    wait_misc_taken(act, MISC[step])
                    ac.copy(parts["x"][:, 0, 0:B * S2], full["x"][:, 0:B * S2]).then_inc(high_ready["x"], 1)
                elif kind == "split_context":
                    act.wait_ge(rest_ready["x"], 1)
                    ac.copy(parts["x"][:, 1, 0:B * S2], full["x"][:, 0:B * S2]).then_inc(middle_ready["x"], 1)
                elif kind == "context_values":
                    if b == 0:
                        wait_cleared(act, "xv_s")
                    ac.copy(xv_s[0:S2, b, :, 0:DH], misc[0:S2, 0:D].rearrange("p (h d) -> p h d", h=H)
                            ).then_inc(taken, 1)
                elif kind == "turn_x":
                    ac.copy(normed_t[k][:], misc).then_inc(taken, 1)
                elif kind in PROJECTED:
                    n = PROJECTED[kind]
                    if n == "x":
                        if b == 0:
                            act.wait_ge(xk_stacked, 16 * N_XK)
                        else:
                            act.wait_ge(stacked["x"][(b - 1) % 2], 16 * STACK_DMAS * ((b + 1) // 2))
                    else:
                        if b == 0:
                            act.wait_ge(first_loaded, 16 * len(FIRST))
                    if n != "x" and b:
                        act.wait_ge(stacked[n][(b - 1) % 2], 16 * STACK_DMAS * ((b + 1) // 2))
                    if n == "x":
                        ac.copy(parts[n][:, 0], misc).then_inc(high_ready[n], 1)
                        ac.copy(full[n][:], misc).then_inc(taken, 1)
                    else:
                        bias = (bq_s if n == "q" else bk_s)[:, 0:1]
                        ac.activation(parts[n][:, 0], misc, ACT.Identity, bias=bias).then_inc(high_ready[n], 1)
                        ac.activation(full[n][:], misc, ACT.Identity, bias=bias).then_inc(taken, 1)
                elif kind in SPLIT:
                    n = SPLIT[kind]
                    act.wait_ge(rest_ready[n], b + (2 if n == "x" else 1))
                    ac.copy(parts[n][:, 1], full[n][:]).then_inc(middle_ready[n], 1)
                elif kind == "turn_peaks":
                    if b:
                        act.wait_ge(max_stacked[k], 32 * b)
                    ac.copy(peaks_t[:, k], misc[0:24, 0:256].bitcast(BF16)).then_inc(taken, 1)
                elif kind == "turn_xpeaks":
                    if b:
                        act.wait_ge(xmax_stacked, 32 * b)
                    ac.copy(xpeaks_t[:], misc[0:48, 0:256].bitcast(BF16)).then_inc(taken, 1)
                elif kind == "scores":
                    grp, u = k
                    act.wait_ge(unit_full, UNIT[step])
                    n = 4 * b + grp
                    if n >= 2:
                        act.wait_ge(values_done, 3 * (n - 1))
                        act.wait_ge(causal_done, 5 * (n - 1))
                    ac.activation(probs[:, grp % 2, u, :], unit_bank(step), ACT.Exp,
                                  scale=SCALE).then_inc(unit_taken[UNIT[step] % UNITS], 1)
                elif kind == "xscores":
                    act.wait_ge(unit_full, UNIT[step])
                    n = H * b + k
                    if n >= XPROBS:
                        act.wait_ge(misc_full, MISC[("xvalues", *divmod((n - XPROBS) // 4, 4))])
                    ac.activation(xprobs[0:S2, n % XPROBS, :], unit_bank(step)[0:S2], ACT.Exp, scale=SCALE
                                  ).then_inc(unit_taken[UNIT[step] % UNITS], 1)
                elif kind == "take_mix":
                    act.wait_ge(values_done, 3 * (4 * b + k + 1))
                    if k or b:
                        act.wait_ge(misc_full, MISC[("mix", b, k - 1) if k else ("mix", b - 1, 3)])
                    ac.copy(mix_t[:, 0], mix_ps[:]).then_inc(mix_taken, 1)
                elif kind == "xvalues":
                    ac.copy(mix_t[:, 1], misc).then_inc(taken, 1)
                elif kind == "turn_mix":
                    ac.copy(mixed_t[:, k], misc).then_inc(taken, 1)
                elif kind == "choose":
                    act.wait_ge(shifted_ready, b + 1)
                    ac.activation(g["exp"][:], g["shifted"][:], ACT.Exp).then_inc(exp_ready, 1)
                elif kind == "turn_gate":
                    ac.copy(comb_t[:], misc[0:T * E, 0:128]).then_inc(taken, 1)

        @block.vector
        def _(dve):
            ve = nc.vector
            chain = [0]

            def link(ins):
                chain[0] += 1
                ins.then_inc(dve_chain, 1)
                dve.wait_ge(dve_chain, chain[0])

            for step in SCHEDULE:
                kind, b, k = step
                if kind in MISC_OF_DVE:
                    dve.wait_ge(misc_full, MISC[step])
                    misc, taken = misc_banks[:, MISC[step] % 2], misc_taken[MISC[step] % 2]
                if kind == "context_keys":
                    dve.wait_ge(rest_loaded, 16 * N_REST)
                    wait_cleared(dve, "rank")
                    ve.tensor_scalar(keep[:], mask_s[:], -1.0, 1.0, ALU.mult, ALU.add)
                    link(ve.tensor_scalar(neg[:], mask_s[:], MASKED, None, ALU.mult))
                    for i in range(2):
                        link(ve.tensor_copy(neg_parts[:, i], neg[:]))
                        link(ve.tensor_tensor(neg[:], neg[:], neg_parts[:, i], ALU.subtract))
                    ve.tensor_copy(neg_parts[:, 2], neg[:]).then_inc(mask_split, 1)
                    ve.tensor_tensor(full["x"][:, 0:B * S2], misc[:, 0:B * S2], keep[:], ALU.mult).then_inc(taken, 1)
                elif kind == "ln_stats":
                    n = 3 * b + k
                    if k == 0:
                        dve.wait_ge(x_loaded[b], 16)
                    for t in range(T):
                        last = ve.bn_stats(stats[:, n, t], state[:, b, t])
                    link(last)
                    for t in range(T):
                        last = ve.bn_aggr(moments[:, n, t], stats[:, n, t])
                    link(last)
                    ve.tensor_scalar(var[:, n], moments[:, n, :, 1], LN_EPS, None, ALU.add).then_inc(var_ready, 1)
                elif kind == "ln_norm":
                    n = 3 * b + k
                    i = NORM[step]
                    dve.wait_ge(rstd_ready, STATS[("ln_stats", b, k)])
                    if i > 2:
                        dve.wait_ge(misc_full, MISC[("turn_x", *NORMS[i - 3][1:])])
                    for t in range(T):
                        last = ve.tensor_scalar(normed[:, i % 2, t], state[:, b, t], moments[:, n, t, 0:1],
                                                rstd[:, n, t:t + 1], ALU.subtract, ALU.mult)
                    last.then_inc(norm_ready, 1)
                    if n == 0:
                        ve.memset(mix_ps[:], 0.0).then_inc(cleared_later, 1)
                        ve.memset(q_stack[:, 1].bitcast(F32), 0.0).then_inc(cleared_later, 1)
                        ve.memset(k_stack[:, 1].bitcast(F32), 0.0).then_inc(cleared_later, 1)
                        ve.memset(xq_stack[:].bitcast(F32), 0.0).then_inc(cleared_later, 1)
                elif kind == "project_v":
                    if b == 0:
                        dve.wait_ge(first_loaded, 16 * len(FIRST))
                        wait_cleared(dve, "v_s")
                    if b >= 2:
                        dve.wait_ge(values_done, 12 * (b - 1))
                    ve.tensor_tensor(v_s[:, b % 2, :, :, 0:DH], misc.rearrange("p (t h d) -> p t h d", t=T, h=H),
                                     bv_s[:].rearrange("p (h d) -> p h d", h=H).unsqueeze(1).broadcast_to([128, T, H, DH]),
                                     ALU.add).then_inc(taken, 1)
                elif kind == "peak":
                    f, u = k
                    t, heads = PEAKS[u]
                    width = 128 * (t + 1)
                    n = sum(1 if s is not None else 2 for _, s in heads)
                    p0, s0 = heads[0]
                    dst = peaks[:, f, t].rearrange("p a s -> p (a s)")[:, 2 * p0 + (s0 or 0):2 * p0 + (s0 or 0) + n]
                    dve.wait_ge(peak_full, PEAK[step])
                    ve.tensor_reduce(dst, peak_bank(step)[:, 0:n * width].rearrange("p (h k) -> p h k", h=n),
                                     X_AXIS, ALU.max, negate=True).then_inc(peak_taken, 1)
                elif kind == "xpeak":
                    t, h, n = XPEAKS[k]
                    dve.wait_ge(peak_full, PEAK[step])
                    ve.tensor_reduce(xpeaks[:, t].rearrange("p a s -> p (a s)")[:, h:h + n],
                                     peak_bank(step)[:, 0:n * S2].rearrange("p (h k) -> p h k", h=n),
                                     X_AXIS, ALU.max, negate=True).then_inc(peak_taken, 1)
                elif kind in ("split_peaks", "split_xpeaks"):
                    if kind == "split_peaks":
                        src, left, dst, done = peaks[:, k], peak_rest[:, k], peak_parts[:, k], peaks_split
                        last_peak = ("peak", b, (k, len(PEAKS) - 1))
                        prior = ("turn_peaks", b - 1, k)
                    else:
                        src, left, dst, done = xpeaks[:], xpeak_rest[:], xpeak_parts[:], xpeaks_split
                        last_peak = ("xpeak", b, len(XPEAKS) - 1)
                        prior = ("turn_xpeaks", b - 1, k)
                    part = [dst[:, :, :, i, :].rearrange("p t s a -> p t a s") for i in range(3)]
                    dve.wait_ge(peak_taken, PEAK[last_peak])
                    if b:
                        dve.wait_ge(misc_full, MISC[prior])
                    link(ve.tensor_copy(part[0], src))
                    link(ve.tensor_tensor(left, src, part[0], ALU.subtract))
                    link(ve.tensor_copy(part[1], left))
                    ve.tensor_tensor(part[2], left, part[1], ALU.subtract).then_inc(done, 1)
                elif kind in ("mix", "xmix"):
                    i = int(kind == "xmix")
                    ps = misc.rearrange("p (t j c) -> p t j c", t=T, j=4)
                    if k == 0 and b:
                        dve.wait_ge(misc_full, MISC[("turn_mix", b - 1, i)])
                    link(ve.reciprocal(share[:, i], ps[:, :, :, DH]))
                    ve.tensor_tensor(mixed[:, i, :, 32 * k:32 * k + 32].rearrange("p t (j d) -> p t j d", j=4),
                                     ps[:, :, :, 0:DH], share[:, i].unsqueeze(3).broadcast_to([128, T, 4, DH]),
                                     ALU.mult).then_inc(taken, 1)
                elif kind == "add_attention":
                    st = state[:, b].rearrange("p t d -> p (t d)")
                    if k == 0:
                        link(ve.tensor_tensor(state[:, b], state[:, b], bp_s[:].unsqueeze(1).broadcast_to([128, T, D]),
                                              ALU.add))
                    ve.tensor_tensor(st, misc, st, ALU.add).then_inc(taken, 1)
                    wait_misc_taken(dve, MISC[step])
                elif kind == "expert_bias":
                    st = state[:, b].rearrange("p t d -> p (t d)")
                    ve.tensor_tensor(st, misc, st, ALU.add).then_inc(taken, 1)
                elif kind == "gate":
                    link(ve.tensor_tensor(g["scores"][:], misc[:, 0:T * E].rearrange("p (t e) -> p t e", t=T),
                                          gate_b_s[:].unsqueeze(1).broadcast_to([128, T, E]), ALU.add))
                    ve.tensor_scalar(g["scores"][:], g["scores"][:], FLOOR, None, ALU.max).then_inc(taken, 1)
                    wait_misc_taken(dve, MISC[step])
                    link(ve.tensor_reduce(g1["max"][:], g["scores"][:], X_AXIS, ALU.max))
                    ve.tensor_tensor(g["shifted"][:], g["scores"][:], wide(g1["max"]), ALU.subtract
                                     ).then_inc(shifted_ready, 1)
                elif kind == "choose":
                    dve.wait_ge(exp_ready, b + 1)
                    if b:
                        dve.wait_ge(misc_full, MISC[("turn_gate", b - 1, 0)])
                    link(ve.tensor_reduce(g1["sum"][:], g["exp"][:], X_AXIS, ALU.add))
                    link(ve.reciprocal(g1["inv"][:], g1["sum"][:]))
                    link(ve.tensor_tensor(g["p"][:], g["exp"][:], wide(g1["inv"]), ALU.mult))
                    for p, top, tied, ranked, best, one in (
                            ("p", "top", "tied", "ranked", "best", "first"),
                            ("left", "top2", "tied2", "ranked2", "best2", "second")):
                        link(ve.tensor_reduce(g1[top][:], g[p][:], X_AXIS, ALU.max))
                        link(ve.tensor_tensor(g[tied][:], g[p][:], wide(g1[top]), ALU.is_ge))
                        link(ve.tensor_tensor(g[ranked][:], g[tied][:], rank[:], ALU.mult))
                        link(ve.tensor_reduce(g1[best][:], g[ranked][:], X_AXIS, ALU.max))
                        link(ve.tensor_tensor(g[one][:], g[ranked][:], wide(g1[best]), ALU.is_ge))
                        if p == "p":
                            link(ve.scalar_tensor_tensor(out=g["left"][:], in0=g["first"][:], scalar=-4.0,
                                                         in1=g["p"][:], op0=ALU.mult, op1=ALU.add))
                    link(ve.tensor_tensor(g["chosen"][:], g["first"][:], g["second"][:], ALU.add))
                    link(ve.tensor_scalar(g["floored"][:], g["p"][:], LEAST_WEIGHT, None, ALU.max))
                    link(ve.tensor_tensor(g["kept"][:], g["floored"][:], g["chosen"][:], ALU.mult))
                    link(ve.tensor_reduce(g1["total"][:], g["kept"][:], X_AXIS, ALU.add))
                    link(ve.reciprocal(g1["inv_total"][:], g1["total"][:]))
                    ve.scalar_tensor_tensor(out=g["comb"][:], in0=g["kept"][:], scalar=1.0 / TOP_K,
                                            in1=wide(g1["inv_total"]), op0=ALU.mult, op1=ALU.mult
                                            ).then_inc(comb_ready, 1)
                    dve.wait_ge(comb_ready, b + 1)
                elif kind == "expert":
                    dve.wait_ge(unit_full, UNIT[step])
                    t, half = divmod(k, 2)
                    n = T * b + t
                    if n >= 2:
                        dve.wait_ge(y_summed, n - 1)
                    ve.tensor_tensor(yw[:, t % 2, 4 * half:4 * half + 4], unit_bank(step).rearrange("p (e d) -> p e d", d=D),
                                     g["comb"][:, t, 4 * half:4 * half + 4].unsqueeze(2).broadcast_to([128, E // 2, D]),
                                     ALU.mult).then_inc(unit_taken[UNIT[step] % UNITS], 1)

        @block.tensor
        def _(pe):
            te = nc.tensor

            def misc_bank(use):
                return misc_banks[:, use % 2]

            def misc_free(use):
                if use > 2:
                    wait_misc_taken(pe, use - 2)

            def unit_free(step):
                n = UNIT[step]
                if n > UNITS:
                    pe.wait_ge(unit_taken[n % UNITS], (n - 1) // UNITS)

            def peak_free(step):
                if PEAK[step] > 2:
                    pe.wait_ge(peak_taken, PEAK[step] - 2)

            def product(weight, moving, use, tiles=False):
                misc_free(use)
                misc = misc_bank(use)
                if not tiles:
                    last = te.matmul(misc, weight[:], moving, start=True, stop=True)
                else:
                    cols = weight.shape[-1]
                    for t in range(T):
                        last = te.matmul(misc[:, cols * t:cols * t + cols], moving[:, 128 * t:128 * t + 128],
                                         weight[:], start=True, stop=True)
                last.then_inc(misc_full, 1)

            for step in SCHEDULE:
                kind, b, k = step
                use = MISC.get(step, 0)
                misc = misc_bank(use)
                if kind == "context_keys":
                    pe.wait_ge(rest_loaded, 16 * N_REST)
                    misc_free(use)
                    te.matmul(misc[:, 0:B * S2], xwk_s[:], ctx_s[:], start=True, stop=True).then_inc(misc_full, 1)
                elif kind == "context_values":
                    misc_free(use)
                    te.matmul(misc[0:S2, 0:D], ctx_s[:, S2 * b:S2 * b + S2], xwv_s[:], start=True, stop=True
                              ).then_inc(misc_full, 1)
                elif kind == "turn_x":
                    i = NORM[("ln_norm", b, k)]
                    if b == 0 and k == 0:
                        wait_cleared(pe, "ident")
                    pe.wait_ge(norm_ready, i)
                    misc_free(use)
                    for t in range(T):
                        last = te.transpose(misc[:, 128 * t:128 * t + 128], normed[:, i % 2, t], ident[:])
                    last.then_inc(misc_full, 1)
                elif kind == "project_q":
                    wait_misc_taken(pe, MISC[("turn_x", b, 0)])
                    if b == 0:
                        pe.wait_ge(first_loaded, 16 * len(FIRST))
                    product(wq_s, normed_t[0][:], use)
                elif kind == "project_k":
                    product(wk_s, normed_t[0][:], use)
                elif kind == "project_v":
                    product(wv_s, normed_t[0], use, tiles=True)
                elif kind == "project_xq":
                    wait_misc_taken(pe, MISC[("turn_x", b, 1)])
                    product(xwq_s, normed_t[1][:], use)
                elif kind == "gate":
                    wait_misc_taken(pe, MISC[("turn_x", b, 2)])
                    product(gate_w_s, normed_t[2], use, tiles=True)
                elif kind == "peak":
                    f, u = k
                    t, heads = PEAKS[u]
                    width = 128 * (t + 1)
                    if u == 0:
                        if b == 0:
                            wait_cleared(pe, "causal")
                        pe.wait_ge(stacked["q"][b % 2], 16 * STACK_DMAS * (b // 2 + 1))
                        pe.wait_ge(stacked["k"][b % 2], 16 * STACK_DMAS * (b // 2 + 1))
                    peak_free(step)
                    bank = peak_bank(step)
                    n = sum(1 if s is not None else 2 for _, s in heads)
                    diagonal = bank[:, 0:n * width].rearrange("p (h k) -> p h k", h=n)[:, :, width - 128:width]
                    te.matmul(diagonal, ident_b[:], causal[:, 0:n], start=True, stop=False, skip_group_check=True)
                    for i, (p, s) in enumerate(heads):
                        q = q_stack[0:MAX_ROW, b % 2, 4 * f + p, 128 * t:128 * t + 128]
                        if s is None:
                            keys = k_stack[0:MAX_ROW, b % 2, :, 4 * f + p, 0:width]
                            dst = bank[:, 2 * width * i:2 * width * (i + 1)].rearrange("p (s k) -> p s k", s=2)
                        else:
                            keys = k_stack[0:MAX_ROW, b % 2, s, 4 * f + p, 0:width]
                            dst = bank[:, 0:width]
                        last = te.matmul(dst, q, keys, start=False, stop=(i == len(heads) - 1), skip_group_check=True)
                    last.then_inc(peak_full, 1)
                elif kind == "xpeak":
                    t, h, n = XPEAKS[k]
                    if k == 0:
                        pe.wait_ge(stacked["x"][b % 2], 16 * STACK_DMAS * (b // 2 + 1))
                        pe.wait_ge(xk_stacked, 16 * N_XK)
                    peak_free(step)
                    for i in range(n):
                        p, s = (h + i) // 2, (h + i) % 2
                        last = te.matmul(peak_bank(step)[:, S2 * i:S2 * i + S2],
                                         xq_stack[0:MAX_ROW, p, 128 * t:128 * t + 128],
                                         xk_stack[0:MAX_ROW, s, p, S2 * b:S2 * b + S2], start=True, stop=True)
                    last.then_inc(peak_full, 1)
                elif kind in ("turn_peaks", "turn_xpeaks"):
                    self_attention = kind == "turn_peaks"
                    src = peak_parts[:, k] if self_attention else xpeak_parts[:]
                    rows = 24 if self_attention else 48
                    pe.wait_ge(peaks_split if self_attention else xpeaks_split, 2 * b + k + 1 if self_attention else b + 1)
                    misc_free(use)
                    for t in range(T):
                        last = te.transpose(misc[0:rows, 64 * t:64 * t + 64].bitcast(BF16),
                                            src[:, t].rearrange("p s i a -> p (s i a)"), ident_b[:])
                    last.then_inc(misc_full, 1)
                elif kind == "scores":
                    grp, u = k
                    if (b, grp, u) == (0, 0, 0):
                        pe.wait_ge(ones_stacked, 16 * 4)
                        pe.wait_ge(cleared_later, 1)
                    if u == 0 and grp % 2 == 0:
                        pe.wait_ge(max_stacked[grp // 2], 32 * (b + 1))
                    unit_free(step)
                    for col, j, kt in SCORES[u]:
                        h = 4 * grp + j
                        p, s = h // 2, h % 2
                        n = S - 128 * kt
                        last = te.matmul(unit_bank(step)[:, col:col + n], k_stack[:, b % 2, s, p, 128 * kt:128 * kt + 128],
                                         q_stack[:, b % 2, p, 128 * kt:S], start=True, stop=True)
                    last.then_inc(unit_full, 1)
                elif kind == "values":
                    grp, v = k
                    tiles, u = VALUES[v]
                    pe.wait_ge(causal_done, 5 * (4 * b + grp) + u + 1)
                    if v == 0:
                        if MIX[("take_mix", b, grp)] > 1:
                            pe.wait_ge(mix_taken, MIX[("take_mix", b, grp)] - 1)
                        wait_misc_taken(pe, MISC[("project_v", b, 0)])
                    for kt in tiles:
                        for j in range(4):
                            unit, col = PLACE[(kt, j)]
                            last = te.matmul(mix_ps[32 * j:32 * j + VW, 128 * kt:S], v_s[:, b % 2, kt, 4 * grp + j],
                                             probs[:, grp % 2, unit, col:col + S - 128 * kt],
                                             start=(kt == 0), stop=(kt == 2), skip_group_check=True)
                    last.then_inc(values_done, 1)
                elif kind == "xscores":
                    if k == 0:
                        pe.wait_ge(xmax_stacked, 32 * (b + 1))
                    unit_free(step)
                    te.matmul(unit_bank(step)[0:S2], xk_stack[:, k % 2, k // 2, S2 * b:S2 * b + S2],
                              xq_stack[:, k // 2], start=True, stop=True).then_inc(unit_full, 1)
                elif kind == "xvalues":
                    for h in range(4 * k, 4 * k + 4):
                        wait_unit_taken(pe, ("xscores", b, h))
                    misc_free(use)
                    for j in range(4):
                        last = te.matmul(misc[32 * j:32 * j + VW, :], xv_s[0:S2, b, 4 * k + j],
                                         xprobs[0:S2, (H * b + 4 * k + j) % XPROBS], start=True, stop=True)
                    last.then_inc(misc_full, 1)
                elif kind in ("mix", "xmix"):
                    i = int(kind == "xmix")
                    if i:
                        wait_misc_taken(pe, MISC[("xvalues", b, k)])
                    else:
                        pe.wait_ge(mix_taken, MIX[("take_mix", b, k)])
                    misc_free(use)
                    for t in range(T):
                        last = te.transpose(misc[:, 128 * t:128 * t + 128], mix_t[:, i, 128 * t:128 * t + 128],
                                            ident[:])
                    last.then_inc(misc_full, 1)
                elif kind == "turn_mix":
                    wait_misc_taken(pe, MISC[("xmix" if k else "mix", b, 3)])
                    misc_free(use)
                    for t in range(T):
                        last = te.transpose(misc[:, 128 * t:128 * t + 128], mixed[:, k, t], ident[:])
                    last.then_inc(misc_full, 1)
                elif kind == "add_attention":
                    wait_misc_taken(pe, MISC[("turn_mix", b, k)])
                    product(xwo_s if k else wp_s, mixed_t[:, k], use, tiles=True)
                elif kind == "turn_gate":
                    pe.wait_ge(comb_ready, b + 1)
                    misc_free(use)
                    te.transpose(misc[0:T * E, 0:128], g["comb"][:].rearrange("p t e -> p (t e)"), ident[:]
                                 ).then_inc(misc_full, 1)
                elif kind == "expert_bias":
                    wait_misc_taken(pe, MISC[("turn_gate", b, 0)])
                    if b == 0:
                        pe.wait_ge(biases_loaded, 16 * T)
                    misc_free(use)
                    for t in range(T):
                        last = te.matmul(misc[:, D * t:D * t + D], comb_t[:], expert_b_s[:, t], start=True, stop=True)
                    last.then_inc(misc_full, 1)
                elif kind == "expert":
                    unit_free(step)
                    t, half = divmod(k, 2)
                    te.matmul(unit_bank(step), normed_t[2][:, 128 * t:128 * t + 128],
                              expert_w_s[:, 4 * half:4 * half + 4].rearrange("d e f -> d (e f)"),
                              start=True, stop=True).then_inc(unit_full, 1)


def kernel(**inputs):
    import concourse.bacc as bacc
    from concourse.bass_utils import run_bass_kernel_spmd

    a = {k: np.asarray(v) for k, v in inputs.items()}

    def by_slot(w):
        return w.reshape(*w.shape[:-1], PAIRS, 2, DH).swapaxes(-3, -2).swapaxes(-2, -1).reshape(w.shape)

    arrays = {
        "x": a["x"],
        "ctx_t": a["ctx_1024"].transpose(2, 0, 1).reshape(D, B * S2),
        "mask": a["mask_Bx1x1xS2_bk0"].reshape(B * S2),
        "wq": by_slot(a["L0_attn_Wq"]), "bq": by_slot(a["L0_attn_bq"]).reshape(D, 1),
        "wk": by_slot(a["L0_attn_Wk"]), "bk": by_slot(a["L0_attn_bk"]).reshape(D, 1),
        "wv": a["L0_attn_Wv"], "bv": a["L0_attn_bv"],
        "wp": a["L0_attn_Wp"], "bp": a["L0_attn_bp"],
        "xwq": by_slot(a["L0_xattn_Wq"].T), "xwk": by_slot(a["L0_xattn_Wk"].T),
        "xwv": a["L0_xattn_Wv"].T, "xwo": a["L0_xattn_Wo"].T,
        "gate_w": a["L0_ffn_gate_W"], "gate_b": a["L0_ffn_gate_b"],
        "expert_w": a["L0_ffn_expert_W"], "expert_b": a["L0_ffn_expert_b"],
    }
    arrays = {k: np.ascontiguousarray(v) for k, v in arrays.items()}
    nc = bacc.Bacc("TRN2", target_bir_lowering=False, num_devices=1)
    args = [nc.dram_tensor(f"in_{k}", v.shape, mybir.dt.from_np(v.dtype), kind="ExternalInput").ap()
            for k, v in arrays.items()]
    out = nc.dram_tensor("out", (B, S, D), F32, kind="ExternalOutput").ap()
    names = list(arrays)
    decoder_layer(nc, **dict(zip(names, args)), out=out)
    r = run_bass_kernel_spmd(nc, [{f"in_{k}": v for k, v in arrays.items()}], core_ids=[0])
    return r.results[0]["out"]
```

```python
from contextlib import ExitStack

import numpy as np

import concourse.bass as bass
from concourse import mybir

F32 = mybir.dt.float32
BF16 = mybir.dt.bfloat16
U8 = mybir.dt.uint8
ALU = mybir.AluOpType
ACT = mybir.ActivationFunctionType
X_AXIS = mybir.AxisListType.X

B, S, D, H, E = 4, 512, 128, 16, 8
DH = D // H
S2 = 77
T = S // 128
PAIRS = H // 2
SCALE = float(1.0 / np.sqrt(np.float32(DH)))
MASKED = -1.0e9
FUTURE = -3.0e38
FLOOR, LEAST_WEIGHT, TOP_K = 1e-4, 0.1, 2
LN_EPS = 1e-5
VW = DH + 1

SLOT_ROWS = 6 * DH
MAX_ROW, ROWS = 96, 102
MASK_ROW, XMAX_ROW, XROWS = 96, 99, 105
Q_PARTS = (0, 0, 0, 1, 1, 2)
K_PARTS = (0, 1, 2, 0, 1, 0)
STACK_DMAS = 2 * len(Q_PARTS)

PEAKS = ([(0, [(p, None) for p in (2 * i, 2 * i + 1)]) for i in range(2)]
         + [(1, [(p, None)]) for p in range(4)]
         + [(t, [(p, s)]) for t in (2, 3) for p in range(4) for s in range(2)])
XPEAKS = [(t, h, n) for t in range(T) for h, n in ((0, 6), (6, 5), (11, 5))]
SCORES = ([[(0, j, 0)] for j in range(4)]
          + [[(0, j, 3), (128, j, 1)] for j in range(4)]
          + [[(0, j, 2), (256, j + 1, 2)] for j in (0, 2)])
PLACE = {(kt, j): (u, col) for u, unit in enumerate(SCORES) for col, j, kt in unit}
VALUES = [((0,), 1), ((1, 3), 3), ((2,), 4)]


XPROBS = 6
UNITS, PEAK_BANKS = 3, 2
SUMMED_BY_DVE = ((B - 1, 1), (B - 1, 3))

COSTS = {
    "ln_stats": (0, "dve", 1.5, 1.4), "ln_norm": (0, "dve", 1.1, 0.24), "turn_x": (0.55, "act", 0.22, 0.11),
    "project_q": (0.72, "act", 1.17, None), "project_k": (0.86, "act", 0.22, None),
    "project_v": (0.55, "dve", 0.95, None), "project_xq": (0.17, "act", 0.19, 3.49),
    "split_q": (0, "act", 0.28, None), "split_k": (0, "act", 0.18, None), "split_xq": (0, "act", 0.7, 5.04),
    "peak": (0.18, "dve", 0.69, None), "split_peaks": (0, "dve", 1.01, 0.25),
    "turn_peaks": (0.57, "act", 0.23, 0.3), "xpeak": (0.19, "dve", 0.49, None),
    "split_xpeaks": (0, "dve", 0.21, 0.71), "turn_xpeaks": (0.13, "act", 0.18, 1.16),
    "scores": (0.31, "act", 0.4, None), "values": (0.9, None, 0, None), "take_mix": (0, "act", 0.5, 0.06),
    "mix": (0.45, "dve", 0.68, None), "turn_mix": (0.24, "act", 0.97, 0.18),
    "add_attention": (0.72, "dve", 0.73, 0.38), "xscores": (0.28, "act", 0.45, None),
    "xvalues": (2.93, "act", 0.5, None), "xmix": (0.24, "dve", 0.88, None), "gate": (0.2, "dve", 0.52, 1.56),
    "choose": (0, "dve", 0.62, None), "turn_gate": (0.05, "act", 0.22, 0.98),
    "expert_bias": (0.19, "dve", 0.25, None), "expert": (1.58, "dve", 0.73, None),
    "sum_experts": (0, "pool", 0.17, None), "context_keys": (0.11, "dve", 3.41, 3.75),
    "split_context": (0, "act", 1.14, None), "context_values": (0.74, "act", 0.1, None),
    "store": (0, None, 0, None)}
DMAS = {"split_q": 12, "split_k": 12, "split_xq": 12, "turn_peaks": 2, "turn_xpeaks": 2, "context_keys": 13,
        "split_context": 12}
DMA_TIME, WARM_TIME, WARM_SLACK, LOADED, HOP = 0.6, 0.48, 0.27, 0.22, 0.08
REST_DELAY, K_DELAY, XQ_DELAY, MAX_DELAY, XMAX_DELAY, CAUSAL_DELAY = 1.1, 0.76, 1.07, 2.89, 2.13, 1.3
VALUES_AFTER = (6, 9, 13)
ORDER = ("cross", "peaks", "experts", "prepare", "attend")


def chains():
    def norm(b, n):
        return [("ln_stats", b, n)] * (b == 0 or n > 0) + [("ln_norm", b, n), ("turn_x", b, n)]

    c = {name: [] for name in ORDER}
    for b in range(B):
        c["prepare"] += norm(b, 0) + [("project_q", b, 0), ("project_k", b, 0), ("split_q", b, 0),
                                      ("project_v", b, 0), ("split_k", b, 0)]
        if b == 0:
            c["prepare"] += [("ln_stats", n, 0) for n in range(1, B)]
            c["prepare"] += [("context_keys", 0, 0), ("split_context", 0, 0)]
            c["prepare"] += [("context_values", n, 0) for n in range(B)]
        for f in range(2):
            c["peaks"] += [("peak", b, (f, u)) for u in range(len(PEAKS))]
            c["peaks"] += [("split_peaks", b, f), ("turn_peaks", b, f)]

        x = [("turn_mix", b, 0), ("add_attention", b, 0)] + norm(b, 1) + [("project_xq", b, 0), ("split_xq", b, 0)]
        x += [("xpeak", b, u) for u in range(len(XPEAKS))] + [("split_xpeaks", b, 0), ("turn_xpeaks", b, 0)]
        x += [("xscores", b, h) for h in range(6)]
        for g in range(4):
            x += [("xvalues", b, g)] + [("xscores", b, h) for h in (4 * g + 6, 4 * g + 7) if h < H]
            x += [("xmix", b, g)] + [("xscores", b, h) for h in (4 * g + 8, 4 * g + 9) if h < H]
        c["cross"] += x + [("turn_mix", b, 1), ("add_attention", b, 1)]

        c["experts"] += norm(b, 2) + [("gate", b, 0), ("choose", b, 0)] + [("expert", b, u) for u in range(UNITS)]
        c["experts"] += [("turn_gate", b, 0), ("expert_bias", b, 0), ("sum_experts", b, 0)]
        for u in range(UNITS, 2 * T):
            c["experts"] += [("expert", b, u)] + [("sum_experts", b, u // 2)] * (u % 2)
        c["experts"] += [("store", b, 0)]

    places = []
    for n in range(4 * B):
        b, g = divmod(n, 4)
        places += [(10 * n + u, 0, ("scores", b, (g, u))) for u in range(len(SCORES))]
        places += [(10 * n + after, v + 1, ("values", b, (g, v))) for v, after in enumerate(VALUES_AFTER)]
        places += [(10 * n + VALUES_AFTER[-1] + i, 4, (kind, b, g)) for i, kind in enumerate(("take_mix", "mix"))]
    c["attend"] = [x for *_, x in sorted(places, key=lambda y: y[:2])]
    return c


def needs(step):
    kind, b, k = step
    if kind == "ln_norm" and k == 0:
        return [(("ln_stats", b, 0), 1.6)] + ([(("values", b - 2, (3, 2)), 0)] if b >= 2 else [])
    if kind in ("split_q", "split_k"):
        return [(("project" + kind[5:], b, 0), REST_DELAY)]
    if kind == "peak" and k == (0, 0):
        return [(("split_k", b, 0), K_DELAY)]
    if kind == "xpeak" and k == 0:
        return [(("split_xq", b, 0), XQ_DELAY), (("split_context", 0, 0), XQ_DELAY)]
    if kind == "turn_peaks" and b:
        return [(("scores", b - 1, (2 * k, 0)), 0)]
    if kind == "scores" and k[0] % 2 == 0 and k[1] == 0:
        return [(("turn_peaks", b, k[0] // 2), MAX_DELAY)]
    if kind == "xscores" and k == 0:
        return [(("turn_xpeaks", b, 0), XMAX_DELAY)]
    if kind == "values":
        g, v = k
        last = [(("take_mix", *divmod(4 * b + g - 1, 4)), 0)] if v == 0 and 4 * b + g else []
        return [(("scores", b, (g, min(2 * VALUES[v][1] + 1, 9))), CAUSAL_DELAY)] + last
    if kind == "xvalues":
        return [(("xscores", b, 4 * k + 3), 0.1)]
    if kind in ("mix", "xmix") and k == 0 and b:
        return [(("turn_mix", b - 1, int(kind == "xmix")), 0)] + ([(("xvalues", b, 0), 0.1)] if kind == "xmix" else [])
    if kind == "xmix":
        return [(("xvalues", b, k), 0.1)]
    if kind == "turn_mix":
        return [(("xmix" if k else "mix", b, 3), 0.1)]
    if kind == "ln_stats" and k == 2:
        return [(("add_attention", b, 1), 0.1)]
    if kind == "turn_gate":
        return [(("choose", b, 0), 0.1)]
    return []


def cost(step):
    kind, b, k = step
    pe, engine, busy, then = COSTS[kind]
    if kind == "peak" and PEAKS[k[1]][0] == 2:
        busy *= 0.75
    elif kind == "values" and k[1] == 2:
        pe *= 0.5
    return pe, engine, busy, then


def plan():
    left = {name: list(steps) for name, steps in chains().items()}
    ready = dict.fromkeys(ORDER, LOADED)
    free = dict.fromkeys(("pe", "act", "dve", "pool", "dma"), 0.0)
    banks = {"misc": [0.0] * 2, "unit": [0.0] * UNITS, "peak": [0.0] * PEAK_BANKS}
    done, turned, norms, steps = {}, set(), [], []
    while any(left.values()):
        best = None
        for rank, name in enumerate(ORDER):
            if not left[name]:
                continue
            step = left[name][0]
            kind = step[0]
            pe, engine, busy, _ = cost(step)
            if any(x not in done for x, _ in needs(step)):
                continue
            if kind == "ln_norm" and len(norms) > 1 and norms[-2] not in turned:
                continue
            start = max([ready[name]] + [done[x] + delay for x, delay in needs(step)])
            ring = ring_of(kind)
            if ring:
                start = max(start, min(banks[ring]))
            start = max(start, free["pe"])
            if best is None or start < best[0]:
                best = (start, name, step, ring)
        start, name, step, ring = best
        kind, b, k = step
        pe, engine, busy, then = cost(step)
        left[name].pop(0)
        idle = int((start - free["pe"] - WARM_SLACK) / WARM_TIME)
        if (("peak", 0, (0, 0)) not in done or ("split_xpeaks", B - 1, 0) in done) and idle > 0:
            steps.append(("warm", len(steps), idle))
        steps.append(step)
        end = start + pe
        if pe:
            free["pe"] = end
        finish = end
        if engine:
            free[engine] = max(end + HOP, free[engine]) + busy
            finish = free[engine] + HOP
        done[step] = finish
        if kind in DMAS:
            begin = done[("project" + kind[5:], b, 0)] - 0.5 if kind in ("split_q", "split_k", "split_xq") else finish
            if kind in ("turn_peaks", "turn_xpeaks"):
                done[step] = begin + 2 * DMA_TIME * DMAS[kind]
                free["dma"] = max(begin, free["dma"]) + DMA_TIME * DMAS[kind]
            else:
                free["dma"] = done[step] = max(begin, free["dma"]) + DMA_TIME * DMAS[kind]
        if ring:
            banks[ring].remove(min(banks[ring]))
            banks[ring].append(finish)
        ready[name] = end if then is None else finish + then
        if kind == "ln_norm":
            norms.append((b, k))
        elif kind == "turn_x":
            turned.add((b, k))
    return steps


MISC_KINDS = ("context_keys", "context_values", "turn_x", "project_q", "project_k", "project_v", "turn_peaks",
              "mix", "turn_mix", "add_attention", "project_xq", "turn_xpeaks", "xvalues", "xmix", "gate",
              "turn_gate", "expert_bias")
UNIT_KINDS, PEAK_KINDS = ("scores", "xscores", "expert"), ("peak", "xpeak")


def ring_of(kind):
    return next((ring for ring, kinds in (("misc", MISC_KINDS), ("unit", UNIT_KINDS), ("peak", PEAK_KINDS))
                 if kind in kinds), None)


SCHEDULE = plan()


def uses(*kinds):
    return {x: n + 1 for n, x in enumerate(x for x in SCHEDULE if x[0] in kinds)}


MISC = uses(*MISC_KINDS)
UNIT = uses(*UNIT_KINDS)
PEAK = uses(*PEAK_KINDS)
MIX = uses("take_mix")
STATS = uses("ln_stats")
NORM = uses("ln_norm")
NORMS = list(NORM)
MISC_OF_ACT = ("turn_x", "project_q", "project_k", "project_xq", "turn_peaks", "turn_xpeaks", "turn_mix",
               "turn_gate", "xvalues", "context_values")
MISC_OF_DVE = ("context_keys", "project_v", "mix", "xmix", "add_attention", "gate", "expert_bias")


def decoder_layer(nc, x, ctx_t, mask, wq, bq, wk, bk, wv, bv, wp, bp, xwq, xwk, xwv, xwo,
                  gate_w, gate_b, expert_w, expert_b, out):
    with ExitStack() as stack:
        def sb(name, shape, dt=F32):
            return stack.enter_context(nc.sbuf_tensor(name, shape, dt))

        def psum(name, shape):
            return stack.enter_context(nc.psum_tensor(name, shape, F32))

        def sem(name):
            return stack.enter_context(nc.semaphore(name))

        peak_ps = psum("peak_ps", [128, PEAK_BANKS, 512])
        unit_ps = psum("unit_ps", [128, UNITS, 512])
        mix_ps = psum("mix_ps", [128, 512])
        misc_banks = psum("misc_banks", [128, 2, 512])

        wq_s, wk_s, wv_s, wp_s, xwq_s, xwk_s, xwv_s, xwo_s = (
            sb(n, [D, D]) for n in ("wq_s", "wk_s", "wv_s", "wp_s", "xwq_s", "xwk_s", "xwv_s", "xwo_s"))
        bq_s, bk_s = sb("bq_s", [D, 1]), sb("bk_s", [D, 1])
        bv_s, bp_s = sb("bv_s", [128, D]), sb("bp_s", [128, D])
        gate_w_s, gate_b_s = sb("gate_w_s", [D, E]), sb("gate_b_s", [128, E])
        expert_w_s = sb("expert_w_s", [D, E, D])
        expert_b_s = sb("expert_b_s", [T * E, T, D])
        ctx_s = sb("ctx_s", [D, B * S2])
        mask_s = sb("mask_s", [128, B * S2], U8)
        ident = sb("ident", [128, 128])
        ident_b = sb("ident_b", [128, 128], BF16)
        causal = sb("causal", [128, 4, 128], BF16)
        ones_b = sb("ones_b", [128, 512], BF16)
        minus_half = sb("minus_half", [128, T])
        rank = sb("rank", [128, T, E])
        keep = sb("keep", [128, B * S2])
        neg = sb("neg", [128, B * S2])
        neg_parts = sb("neg_parts", [128, 3, B * S2], BF16)

        state = sb("state", [128, B, T, D])
        stats = sb("stats", [128, 3 * B, T, 6])
        moments = sb("moments", [128, 3 * B, T, 2])
        var = sb("var", [128, 3 * B, T])
        rstd = sb("rstd", [128, 3 * B, T])
        normed = sb("normed", [128, 2, T, D])
        normed_t = [sb(f"normed_t{n}", [D, S]) for n in range(3)]

        kinds = ("q", "k", "x")
        full = {n: sb(f"full_{n}", [D, S]) for n in kinds}
        parts = {n: sb(f"parts_{n}", [D, 3, S], BF16) for n in kinds}
        q_stack = sb("q_stack", [128, 2, PAIRS, S], BF16)
        k_stack = sb("k_stack", [128, 2, 2, PAIRS, S], BF16)
        xq_stack = sb("xq_stack", [128, PAIRS, S], BF16)
        xk_stack = sb("xk_stack", [128, 2, PAIRS, B * S2], BF16)
        v_s = sb("v_s", [128, 2, T, H, VW])
        xv_s = sb("xv_s", [128, B, H, VW])

        peaks = sb("peaks", [128, 2, T, 4, 2])
        peak_rest = sb("peak_rest", [128, 2, T, 4, 2])
        peak_parts = sb("peak_parts", [128, 2, T, 2, 3, 4], BF16)
        peaks_t = sb("peaks_t", [24, 2, S], BF16)
        xpeaks = sb("xpeaks", [128, T, PAIRS, 2])
        xpeak_rest = sb("xpeak_rest", [128, T, PAIRS, 2])
        xpeak_parts = sb("xpeak_parts", [128, T, 2, 3, PAIRS], BF16)
        xpeaks_t = sb("xpeaks_t", [48, S], BF16)

        probs = sb("probs", [128, 2, 10, 512])
        xprobs = sb("xprobs", [128, XPROBS, 512])
        mix_t = sb("mix_t", [128, 2, 512])
        share = sb("share", [128, 2, T, 4])
        mixed = sb("mixed", [128, 2, T, D])
        mixed_t = sb("mixed_t", [D, 2, S])

        g = {n: sb(f"g_{n}", [128, T, E]) for n in
             ("scores", "shifted", "exp", "p", "tied", "ranked", "first", "left", "tied2", "ranked2",
              "second", "chosen", "floored", "kept", "comb")}
        g1 = {n: sb(f"g1_{n}", [128, T]) for n in
              ("max", "sum", "inv", "top", "best", "top2", "best2", "total", "inv_total")}
        comb_t = sb("comb_t", [T * E, 128])
        yw = sb("yw", [128, 2, E, D])
        y_total = sb("y_total", [128, D])

        x_loaded = [sem(f"x_loaded{b}") for b in range(B)]
        first_loaded = sem("first_loaded")
        rest_loaded = sem("rest_loaded")
        biases_loaded = sem("biases_loaded")
        cleared = sem("cleared")
        cleared_later = sem("cleared_later")
        ones_stacked = sem("ones_stacked")
        mask_split = sem("mask_split")
        var_ready, rstd_ready, norm_ready = sem("var_ready"), sem("rstd_ready"), sem("norm_ready")
        misc_full = sem("misc_full")
        misc_taken = [sem("misc_taken0"), sem("misc_taken1")]
        unit_full = sem("unit_full")
        unit_taken = [sem(f"unit_taken{i}") for i in range(UNITS)]
        peak_full, peak_taken = sem("peak_full"), sem("peak_taken")
        mix_taken = sem("mix_taken")
        high_ready = {n: sem(f"high_ready_{n}") for n in kinds}
        rest_ready = {n: sem(f"rest_ready_{n}") for n in kinds}
        middle_ready = {n: sem(f"middle_ready_{n}") for n in kinds}
        low_ready = {n: sem(f"low_ready_{n}") for n in kinds}
        stacked = {n: [sem(f"stacked_{n}{i}") for i in range(2)] for n in kinds}
        xk_stacked = sem("xk_stacked")
        peaks_split, xpeaks_split = sem("peaks_split"), sem("xpeaks_split")
        max_stacked = [sem("max_stacked0"), sem("max_stacked1")]
        xmax_stacked = sem("xmax_stacked")
        causal_done = sem("causal_done")
        values_done = sem("values_done")
        shifted_ready, exp_ready, comb_ready = sem("shifted_ready"), sem("exp_ready"), sem("comb_ready")
        y_summed, y_summed_by_dve = sem("y_summed"), sem("y_summed_by_dve")
        stored = sem("stored")
        dve_chain, pool_chain = sem("dve_chain"), sem("pool_chain")

        block = stack.enter_context(nc.Block())

        FIRST = [(wq_s[:], wq), (bq_s[:], bq), (wk_s[:], wk), (bk_s[:], bk), (wv_s[:], wv),
                 (bv_s[:], bv.partition_broadcast(128))]
        REST = [(xwk_s[:], xwk), (ctx_s[:], ctx_t), (mask_s[:], mask.partition_broadcast(128)), (xwv_s[:], xwv),
                (wp_s[:], wp), (bp_s[:], bp.partition_broadcast(128)), (xwq_s[:], xwq), (xwo_s[:], xwo),
                (gate_w_s[:], gate_w), (gate_b_s[:], gate_b.partition_broadcast(128)),
                (expert_w_s[:], expert_w.rearrange("e d f -> d e f"))]
        N_REST = len(REST)
        CLEARED = ["ones_b", "minus_half", "ident", "k_stack", "causal", "v_s", "xk_stack", "xv_s", "expert_b_s",
                   "rank"]

        N_XK = STACK_DMAS + 3 + 6

        def wait_cleared(eng, name):
            eng.wait_ge(cleared, CLEARED.index(name) + 1)

        PROJECTED = {"project_q": "q", "project_k": "k", "project_xq": "x"}
        SPLIT = {"split_q": "q", "split_k": "k", "split_xq": "x"}

        def wide(a):
            return a[:].unsqueeze(2).broadcast_to([128, T, E])

        def wait_misc_taken(eng, use):
            eng.wait_ge(misc_taken[use % 2], (use + 1) // 2)

        def wait_unit_taken(eng, step):
            eng.wait_ge(unit_taken[UNIT[step] % UNITS], (UNIT[step] + UNITS - 1) // UNITS)

        def summed_by_pool(n):
            return sum(divmod(m, T) not in SUMMED_BY_DVE for m in range(n))

        def peak_bank(step):
            return peak_ps[:, PEAK[step] % PEAK_BANKS, :]

        def unit_bank(step):
            return unit_ps[:, UNIT[step] % UNITS]

        @block.sync
        def _(sp):
            for b in range(B):
                sp.dma_start(state[:, b], x[b].rearrange("(t p) d -> p t d", p=128)).then_inc(x_loaded[b], 16)
                if b == 0:
                    for dst, src in FIRST:
                        sp.dma_start(dst, src).then_inc(first_loaded, 16)
            for dst, src in REST:
                sp.dma_start(dst, src).then_inc(rest_loaded, 16)
            ones = ones_b[0:3 * PAIRS, :]

            def stack_free(b):
                if b >= 2:
                    sp.wait_ge(values_done, 12 * (b - 1))

            def copy_parts(n, nth, order, rows, cols, done):
                for part, ready in enumerate((high_ready[n], middle_ready[n], low_ready[n])):
                    sp.wait_ge(ready, nth)
                    for i in range(len(order)):
                        if order[i] == part:
                            for s in range(2):
                                sp.dma_start(rows(SLOT_ROWS * s + DH * i, s),
                                             parts[n][64 * s:64 * s + 64, part, 0:cols]).then_inc(done, 16)

            for step in SCHEDULE:
                kind, b, k = step
                if kind == "peak" and (b, k) == (0, (0, 0)):
                    wait_cleared(sp, "k_stack")
                    sp.wait_ge(cleared_later, 3)
                    for i in range(2):
                        for s in range(2):
                            r = MAX_ROW + 3 * s
                            sp.dma_start(k_stack[r:r + 3, i, s], ones).then_inc(ones_stacked, 16)
                elif kind == "context_keys":
                    wait_cleared(sp, "expert_b_s")
                    for t in range(T):
                        sp.dma_start(expert_b_s[E * t:E * t + E, t, :], expert_b).then_inc(biases_loaded, 16)
                    sp.dma_start(xq_stack[MASK_ROW:MASK_ROW + 3], ones).then_inc(xk_stacked, 16)
                    for s in range(2):
                        r = XMAX_ROW + 3 * s
                        sp.dma_start(xk_stack[r:r + 3, s], ones_b[0:3 * PAIRS, 0:B * S2]).then_inc(xk_stacked, 16)
                    sp.wait_ge(mask_split, 1)
                    for s in range(2):
                        for i in range(3):
                            sp.dma_start(xk_stack[MASK_ROW + i:MASK_ROW + i + 1, s],
                                         neg_parts[0:1, i].unsqueeze(1).broadcast_to([1, PAIRS, B * S2])
                                         ).then_inc(xk_stacked, 16)
                elif kind == "split_context":
                    copy_parts("x", 1, K_PARTS, lambda r, s: xk_stack[r:r + DH, s], B * S2, xk_stacked)
                elif kind == "split_q":
                    stack_free(b)
                    copy_parts("q", b + 1, Q_PARTS, lambda r, s: q_stack[r:r + DH, b % 2], S, stacked["q"][b % 2])
                elif kind == "split_k":
                    if b == 0:
                        wait_cleared(sp, "k_stack")
                        sp.wait_ge(cleared_later, 1)
                    elif b == 1:
                        sp.wait_ge(cleared_later, 3)
                    stack_free(b)
                    copy_parts("k", b + 1, K_PARTS, lambda r, s: k_stack[r:r + DH, b % 2, s], S, stacked["k"][b % 2])
                elif kind == "split_xq":
                    if b >= 1:
                        sp.wait_ge(misc_full, MISC[("xvalues", b - 1, 3)])
                    copy_parts("x", b + 2, Q_PARTS, lambda r, s: xq_stack[r:r + DH], S, stacked["x"][b % 2])
                elif kind == "store":
                    sp.wait_ge(y_summed, summed_by_pool(T * (b + 1)))
                    if b == B - 1:
                        sp.wait_ge(y_summed_by_dve, len(SUMMED_BY_DVE))
                    sp.dma_start(out[b].rearrange("(t p) d -> p t d", p=128), state[:, b]).then_inc(stored, 16)
            sp.wait_ge(stored, 16 * B)

        @block.gpsimd
        def _(pool):
            gp = nc.gpsimd
            chain = [0]

            def link(ins):
                chain[0] += 1
                ins.then_inc(pool_chain, 1)
                pool.wait_ge(pool_chain, chain[0])

            def clear(buffer):
                v = buffer[:] if buffer.dtype == F32 else buffer[:].bitcast(F32)
                return gp.memset(v, 0.0)

            gp.memset(ones_b[:], 1.0).then_inc(cleared, 1)
            gp.memset(minus_half[:], -0.5).then_inc(cleared, 1)
            link(gp.memset(ident[:], 0.0))
            link(gp.affine_select(out=ident[:], in_=ident[:], compare_op=ALU.not_equal, fill=1.0, base=0,
                                  pattern=[[-1, 128]], channel_multiplier=1))
            gp.tensor_copy(ident_b[:], ident[:]).then_inc(cleared, 1)

            def leave_rest(n, use, cols):
                wait_misc_taken(pool, use)
                gp.tensor_tensor(full[n][:, 0:cols], full[n][:, 0:cols], parts[n][:, 0, 0:cols],
                                 ALU.subtract).then_inc(rest_ready[n], 1)

            def low_part(n, cols, nth):
                pool.wait_ge(middle_ready[n], nth)
                gp.tensor_tensor(parts[n][:, 2, 0:cols], full[n][:, 0:cols], parts[n][:, 1, 0:cols],
                                 ALU.subtract).then_inc(low_ready[n], 1)

            for step in SCHEDULE:
                kind, b, k = step
                if kind == "ln_stats":
                    n = 3 * b + k
                    pool.wait_ge(var_ready, STATS[step])
                    if n == 0:
                        wait_cleared(pool, "minus_half")
                    gp.tensor_tensor(rstd[:, n], var[:, n], minus_half[:], ALU.pow).then_inc(rstd_ready, 1)
                    if n == 0:
                        gp.memset(k_stack[:, 0, 0].bitcast(F32), 0.0).then_inc(cleared, 1)
                        link(gp.memset(causal[:], 0.0))
                        gp.affine_select(out=causal[:], in_=causal[:], compare_op=ALU.is_ge, fill=FUTURE, base=0,
                                         pattern=[[0, 4], [-1, 128]], channel_multiplier=1).then_inc(cleared, 1)
                        link(clear(v_s))
                        gp.memset(v_s[:, :, :, :, DH:DH + 1], 1.0).then_inc(cleared, 1)
                elif kind in PROJECTED:
                    leave_rest(PROJECTED[kind], MISC[step], S)
                elif kind in SPLIT:
                    low_part(SPLIT[kind], S, b + (2 if kind == "split_xq" else 1))
                    if kind == "split_k" and b == 0:
                        clear(xk_stack).then_inc(cleared, 1)
                        gp.memset(xv_s[:, :, :, DH:DH + 1], 1.0).then_inc(cleared, 1)
                        clear(expert_b_s).then_inc(cleared, 1)
                        for e in range(E):
                            last = gp.memset(rank[:, :, e:e + 1], float(E - e))
                        last.then_inc(cleared, 1)
                elif kind == "context_keys":
                    pool.wait_ge(high_ready["x"], 1)
                    gp.tensor_tensor(full["x"][:, 0:B * S2], full["x"][:, 0:B * S2], parts["x"][:, 0, 0:B * S2],
                                     ALU.subtract).then_inc(rest_ready["x"], 1)
                elif kind == "split_context":
                    low_part("x", B * S2, 1)
                elif kind == "scores":
                    grp, u = k
                    if u % 2 == 0:
                        continue
                    wait_unit_taken(pool, step)
                    p = probs[:, grp % 2, u - 1:u + 1, :]
                    if u < 4:
                        v, pattern = p[:, :, 0:128], [[0, 2], [1, 128]]
                    elif u < 8:
                        v, pattern = p[:, :, 0:256], [[0, 2], [0, 2], [1, 128]]
                    else:
                        v, pattern = p.rearrange("p b (c q) -> p (b c) q", q=256)[:, :, 0:128], [[0, 4], [1, 128]]
                    gp.affine_select(out=v, in_=v, compare_op=ALU.is_ge, fill=0.0, base=0, pattern=pattern,
                                     channel_multiplier=-1).then_inc(causal_done, 1)
                elif kind == "sum_experts" and (b, k) not in SUMMED_BY_DVE:
                    t = k
                    wait_unit_taken(pool, ("expert", b, 2 * t))
                    wait_unit_taken(pool, ("expert", b, 2 * t + 1))
                    if T * b + t:
                        pool.wait_ge(y_summed, summed_by_pool(T * b + t))
                    y = yw[:, t % 2]
                    for n in (4, 2, 1):
                        link(gp.tensor_tensor(y[:, 0:n], y[:, 0:n], y[:, n:2 * n], ALU.add))
                    if t == 0:
                        wait_misc_taken(pool, MISC[("expert_bias", b, 0)])
                    gp.tensor_tensor(state[:, b, t], y[:, 0], state[:, b, t], ALU.add).then_inc(y_summed, 1)

        @block.scalar
        def _(act):
            ac = nc.scalar

            for step in SCHEDULE:
                kind, b, k = step
                if kind in MISC_OF_ACT:
                    act.wait_ge(misc_full, MISC[step])
                    misc, taken = misc_banks[:, MISC[step] % 2], misc_taken[MISC[step] % 2]
                if kind == "context_keys":
                    wait_misc_taken(act, MISC[step])
                    ac.copy(parts["x"][:, 0, 0:B * S2], full["x"][:, 0:B * S2]).then_inc(high_ready["x"], 1)
                elif kind == "split_context":
                    act.wait_ge(rest_ready["x"], 1)
                    ac.copy(parts["x"][:, 1, 0:B * S2], full["x"][:, 0:B * S2]).then_inc(middle_ready["x"], 1)
                elif kind == "context_values":
                    if b == 0:
                        wait_cleared(act, "xv_s")
                    ac.copy(xv_s[0:S2, b, :, 0:DH], misc[0:S2, 0:D].rearrange("p (h d) -> p h d", h=H)
                            ).then_inc(taken, 1)
                elif kind == "turn_x":
                    ac.copy(normed_t[k][:], misc).then_inc(taken, 1)
                elif kind in PROJECTED:
                    n = PROJECTED[kind]
                    if n == "x":
                        if b == 0:
                            act.wait_ge(xk_stacked, 16 * N_XK)
                        else:
                            act.wait_ge(stacked["x"][(b - 1) % 2], 16 * STACK_DMAS * ((b + 1) // 2))
                    else:
                        if b == 0:
                            act.wait_ge(first_loaded, 16 * len(FIRST))
                    if n != "x" and b:
                        act.wait_ge(stacked[n][(b - 1) % 2], 16 * STACK_DMAS * ((b + 1) // 2))
                    if n == "x":
                        ac.copy(parts[n][:, 0], misc).then_inc(high_ready[n], 1)
                        ac.copy(full[n][:], misc).then_inc(taken, 1)
                    else:
                        bias = (bq_s if n == "q" else bk_s)[:, 0:1]
                        ac.activation(parts[n][:, 0], misc, ACT.Identity, bias=bias).then_inc(high_ready[n], 1)
                        ac.activation(full[n][:], misc, ACT.Identity, bias=bias).then_inc(taken, 1)
                elif kind in SPLIT:
                    n = SPLIT[kind]
                    act.wait_ge(rest_ready[n], b + (2 if n == "x" else 1))
                    ac.copy(parts[n][:, 1], full[n][:]).then_inc(middle_ready[n], 1)
                elif kind == "turn_peaks":
                    if b:
                        act.wait_ge(max_stacked[k], 32 * b)
                    ac.copy(peaks_t[:, k], misc[0:24, 0:256].bitcast(BF16)).then_inc(taken, 1)
                    wait_misc_taken(act, MISC[step])
                    for s in range(2):
                        r = MAX_ROW + 3 * s
                        act.dma_start(q_stack[r:r + 3, b % 2, 4 * k:4 * k + 4],
                                      peaks_t[12 * s:12 * s + 12, k]).then_inc(max_stacked[k], 16)
                elif kind == "turn_xpeaks":
                    if b:
                        act.wait_ge(xmax_stacked, 32 * b)
                    ac.copy(xpeaks_t[:], misc[0:48, 0:256].bitcast(BF16)).then_inc(taken, 1)
                    wait_misc_taken(act, MISC[step])
                    for s in range(2):
                        r = XMAX_ROW + 3 * s
                        act.dma_start(xq_stack[r:r + 3], xpeaks_t[24 * s:24 * s + 24, :]).then_inc(xmax_stacked, 16)
                elif kind == "scores":
                    grp, u = k
                    act.wait_ge(unit_full, UNIT[step])
                    n = 4 * b + grp
                    if n >= 2:
                        act.wait_ge(values_done, 3 * (n - 1))
                        act.wait_ge(causal_done, 5 * (n - 1))
                    ac.activation(probs[:, grp % 2, u, :], unit_bank(step), ACT.Exp,
                                  scale=SCALE).then_inc(unit_taken[UNIT[step] % UNITS], 1)
                elif kind == "xscores":
                    act.wait_ge(unit_full, UNIT[step])
                    n = H * b + k
                    if n >= XPROBS:
                        act.wait_ge(misc_full, MISC[("xvalues", *divmod((n - XPROBS) // 4, 4))])
                    ac.activation(xprobs[0:S2, n % XPROBS, :], unit_bank(step)[0:S2], ACT.Exp, scale=SCALE
                                  ).then_inc(unit_taken[UNIT[step] % UNITS], 1)
                elif kind == "take_mix":
                    act.wait_ge(values_done, 3 * (4 * b + k + 1))
                    if k or b:
                        act.wait_ge(misc_full, MISC[("mix", b, k - 1) if k else ("mix", b - 1, 3)])
                    ac.copy(mix_t[:, 0], mix_ps[:]).then_inc(mix_taken, 1)
                elif kind == "xvalues":
                    ac.copy(mix_t[:, 1], misc).then_inc(taken, 1)
                elif kind == "turn_mix":
                    ac.copy(mixed_t[:, k], misc).then_inc(taken, 1)
                elif kind == "choose":
                    act.wait_ge(shifted_ready, b + 1)
                    ac.activation(g["exp"][:], g["shifted"][:], ACT.Exp).then_inc(exp_ready, 1)
                elif kind == "turn_gate":
                    ac.copy(comb_t[:], misc[0:T * E, 0:128]).then_inc(taken, 1)

        @block.vector
        def _(dve):
            ve = nc.vector
            chain = [0]

            def link(ins):
                chain[0] += 1
                ins.then_inc(dve_chain, 1)
                dve.wait_ge(dve_chain, chain[0])

            for step in SCHEDULE:
                kind, b, k = step
                if kind in MISC_OF_DVE:
                    dve.wait_ge(misc_full, MISC[step])
                    misc, taken = misc_banks[:, MISC[step] % 2], misc_taken[MISC[step] % 2]
                if kind == "context_keys":
                    dve.wait_ge(rest_loaded, 16 * N_REST)
                    wait_cleared(dve, "rank")
                    ve.tensor_scalar(keep[:], mask_s[:], -1.0, 1.0, ALU.mult, ALU.add)
                    link(ve.tensor_scalar(neg[:], mask_s[:], MASKED, None, ALU.mult))
                    for i in range(2):
                        link(ve.tensor_copy(neg_parts[:, i], neg[:]))
                        link(ve.tensor_tensor(neg[:], neg[:], neg_parts[:, i], ALU.subtract))
                    ve.tensor_copy(neg_parts[:, 2], neg[:]).then_inc(mask_split, 1)
                    ve.tensor_tensor(full["x"][:, 0:B * S2], misc[:, 0:B * S2], keep[:], ALU.mult).then_inc(taken, 1)
                elif kind == "ln_stats":
                    n = 3 * b + k
                    if k == 0:
                        dve.wait_ge(x_loaded[b], 16)
                    for t in range(T):
                        last = ve.bn_stats(stats[:, n, t], state[:, b, t])
                    link(last)
                    for t in range(T):
                        last = ve.bn_aggr(moments[:, n, t], stats[:, n, t])
                    link(last)
                    ve.tensor_scalar(var[:, n], moments[:, n, :, 1], LN_EPS, None, ALU.add).then_inc(var_ready, 1)
                elif kind == "ln_norm":
                    n = 3 * b + k
                    i = NORM[step]
                    dve.wait_ge(rstd_ready, STATS[("ln_stats", b, k)])
                    if i > 2:
                        dve.wait_ge(misc_full, MISC[("turn_x", *NORMS[i - 3][1:])])
                    for t in range(T):
                        last = ve.tensor_scalar(normed[:, i % 2, t], state[:, b, t], moments[:, n, t, 0:1],
                                                rstd[:, n, t:t + 1], ALU.subtract, ALU.mult)
                    last.then_inc(norm_ready, 1)
                    if n == 0:
                        ve.memset(k_stack[:, 0, 1].bitcast(F32), 0.0).then_inc(cleared_later, 1)
                        ve.memset(mix_ps[:], 0.0).then_inc(cleared_later, 1)
                        ve.memset(k_stack[:, 1].bitcast(F32), 0.0).then_inc(cleared_later, 1)
                elif kind == "project_v":
                    if b == 0:
                        dve.wait_ge(first_loaded, 16 * len(FIRST))
                        wait_cleared(dve, "v_s")
                    if b >= 2:
                        dve.wait_ge(values_done, 12 * (b - 1))
                    ve.tensor_tensor(v_s[:, b % 2, :, :, 0:DH], misc.rearrange("p (t h d) -> p t h d", t=T, h=H),
                                     bv_s[:].rearrange("p (h d) -> p h d", h=H).unsqueeze(1).broadcast_to([128, T, H, DH]),
                                     ALU.add).then_inc(taken, 1)
                elif kind == "peak":
                    f, u = k
                    t, heads = PEAKS[u]
                    width = 128 * (t + 1)
                    n = sum(1 if s is not None else 2 for _, s in heads)
                    p0, s0 = heads[0]
                    dst = peaks[:, f, t].rearrange("p a s -> p (a s)")[:, 2 * p0 + (s0 or 0):2 * p0 + (s0 or 0) + n]
                    dve.wait_ge(peak_full, PEAK[step])
                    ve.tensor_reduce(dst, peak_bank(step)[:, 0:n * width].rearrange("p (h k) -> p h k", h=n),
                                     X_AXIS, ALU.max, negate=True).then_inc(peak_taken, 1)
                elif kind == "xpeak":
                    t, h, n = XPEAKS[k]
                    dve.wait_ge(peak_full, PEAK[step])
                    ve.tensor_reduce(xpeaks[:, t].rearrange("p a s -> p (a s)")[:, h:h + n],
                                     peak_bank(step)[:, 0:n * S2].rearrange("p (h k) -> p h k", h=n),
                                     X_AXIS, ALU.max, negate=True).then_inc(peak_taken, 1)
                elif kind in ("split_peaks", "split_xpeaks"):
                    if kind == "split_peaks":
                        src, left, dst, done = peaks[:, k], peak_rest[:, k], peak_parts[:, k], peaks_split
                        last_peak = ("peak", b, (k, len(PEAKS) - 1))
                        prior = ("turn_peaks", b - 1, k)
                    else:
                        src, left, dst, done = xpeaks[:], xpeak_rest[:], xpeak_parts[:], xpeaks_split
                        last_peak = ("xpeak", b, len(XPEAKS) - 1)
                        prior = ("turn_xpeaks", b - 1, k)
                    part = [dst[:, :, :, i, :].rearrange("p t s a -> p t a s") for i in range(3)]
                    dve.wait_ge(peak_taken, PEAK[last_peak])
                    if b:
                        dve.wait_ge(misc_full, MISC[prior])
                    link(ve.tensor_copy(part[0], src))
                    link(ve.tensor_tensor(left, src, part[0], ALU.subtract))
                    link(ve.tensor_copy(part[1], left))
                    ve.tensor_tensor(part[2], left, part[1], ALU.subtract).then_inc(done, 1)
                elif kind in ("mix", "xmix"):
                    i = int(kind == "xmix")
                    ps = misc.rearrange("p (t j c) -> p t j c", t=T, j=4)
                    if k == 0 and b:
                        dve.wait_ge(misc_full, MISC[("turn_mix", b - 1, i)])
                    link(ve.reciprocal(share[:, i], ps[:, :, :, DH]))
                    ve.tensor_tensor(mixed[:, i, :, 32 * k:32 * k + 32].rearrange("p t (j d) -> p t j d", j=4),
                                     ps[:, :, :, 0:DH], share[:, i].unsqueeze(3).broadcast_to([128, T, 4, DH]),
                                     ALU.mult).then_inc(taken, 1)
                elif kind == "add_attention":
                    st = state[:, b].rearrange("p t d -> p (t d)")
                    if k == 0:
                        link(ve.tensor_tensor(state[:, b], state[:, b], bp_s[:].unsqueeze(1).broadcast_to([128, T, D]),
                                              ALU.add))
                    ve.tensor_tensor(st, misc, st, ALU.add).then_inc(taken, 1)
                    wait_misc_taken(dve, MISC[step])
                elif kind == "expert_bias":
                    st = state[:, b].rearrange("p t d -> p (t d)")
                    ve.tensor_tensor(st, misc, st, ALU.add).then_inc(taken, 1)
                elif kind == "gate":
                    link(ve.tensor_tensor(g["scores"][:], misc[:, 0:T * E].rearrange("p (t e) -> p t e", t=T),
                                          gate_b_s[:].unsqueeze(1).broadcast_to([128, T, E]), ALU.add))
                    ve.tensor_scalar(g["scores"][:], g["scores"][:], FLOOR, None, ALU.max).then_inc(taken, 1)
                    wait_misc_taken(dve, MISC[step])
                    link(ve.tensor_reduce(g1["max"][:], g["scores"][:], X_AXIS, ALU.max))
                    ve.tensor_tensor(g["shifted"][:], g["scores"][:], wide(g1["max"]), ALU.subtract
                                     ).then_inc(shifted_ready, 1)
                elif kind == "choose":
                    dve.wait_ge(exp_ready, b + 1)
                    if b:
                        dve.wait_ge(misc_full, MISC[("turn_gate", b - 1, 0)])
                    link(ve.tensor_reduce(g1["sum"][:], g["exp"][:], X_AXIS, ALU.add))
                    link(ve.reciprocal(g1["inv"][:], g1["sum"][:]))
                    link(ve.tensor_tensor(g["p"][:], g["exp"][:], wide(g1["inv"]), ALU.mult))
                    for p, top, tied, ranked, best, one in (
                            ("p", "top", "tied", "ranked", "best", "first"),
                            ("left", "top2", "tied2", "ranked2", "best2", "second")):
                        link(ve.tensor_reduce(g1[top][:], g[p][:], X_AXIS, ALU.max))
                        link(ve.tensor_tensor(g[tied][:], g[p][:], wide(g1[top]), ALU.is_ge))
                        link(ve.tensor_tensor(g[ranked][:], g[tied][:], rank[:], ALU.mult))
                        link(ve.tensor_reduce(g1[best][:], g[ranked][:], X_AXIS, ALU.max))
                        link(ve.tensor_tensor(g[one][:], g[ranked][:], wide(g1[best]), ALU.is_ge))
                        if p == "p":
                            link(ve.scalar_tensor_tensor(out=g["left"][:], in0=g["first"][:], scalar=-4.0,
                                                         in1=g["p"][:], op0=ALU.mult, op1=ALU.add))
                    link(ve.tensor_tensor(g["chosen"][:], g["first"][:], g["second"][:], ALU.add))
                    link(ve.tensor_scalar(g["floored"][:], g["p"][:], LEAST_WEIGHT, None, ALU.max))
                    link(ve.tensor_tensor(g["kept"][:], g["floored"][:], g["chosen"][:], ALU.mult))
                    link(ve.tensor_reduce(g1["total"][:], g["kept"][:], X_AXIS, ALU.add))
                    link(ve.reciprocal(g1["inv_total"][:], g1["total"][:]))
                    ve.scalar_tensor_tensor(out=g["comb"][:], in0=g["kept"][:], scalar=1.0 / TOP_K,
                                            in1=wide(g1["inv_total"]), op0=ALU.mult, op1=ALU.mult
                                            ).then_inc(comb_ready, 1)
                    dve.wait_ge(comb_ready, b + 1)
                elif kind == "expert":
                    dve.wait_ge(unit_full, UNIT[step])
                    t, half = divmod(k, 2)
                    n = T * b + t
                    if n >= 2:
                        dve.wait_ge(y_summed, summed_by_pool(n - 1))
                    ve.tensor_tensor(yw[:, t % 2, 4 * half:4 * half + 4], unit_bank(step).rearrange("p (e d) -> p e d", d=D),
                                     g["comb"][:, t, 4 * half:4 * half + 4].unsqueeze(2).broadcast_to([128, E // 2, D]),
                                     ALU.mult).then_inc(unit_taken[UNIT[step] % UNITS], 1)
                elif kind == "sum_experts" and (b, k) in SUMMED_BY_DVE:
                    wait_unit_taken(dve, ("expert", b, 2 * k))
                    wait_unit_taken(dve, ("expert", b, 2 * k + 1))
                    link(ve.tensor_reduce(y_total[:], yw[:, k % 2].rearrange("p e d -> p d e"), X_AXIS, ALU.add))
                    ve.tensor_tensor(state[:, b, k], y_total[:], state[:, b, k], ALU.add
                                     ).then_inc(y_summed_by_dve, 1)

        @block.tensor
        def _(pe):
            te = nc.tensor

            def misc_bank(use):
                return misc_banks[:, use % 2]

            def misc_free(use):
                if use > 2:
                    wait_misc_taken(pe, use - 2)

            def unit_free(step):
                n = UNIT[step]
                if n > UNITS:
                    pe.wait_ge(unit_taken[n % UNITS], (n - 1) // UNITS)

            def peak_free(step):
                if PEAK[step] > PEAK_BANKS:
                    pe.wait_ge(peak_taken, PEAK[step] - PEAK_BANKS)

            def product(weight, moving, use, tiles=False):
                misc_free(use)
                misc = misc_bank(use)
                if not tiles:
                    last = te.matmul(misc, weight[:], moving, start=True, stop=True)
                else:
                    cols = weight.shape[-1]
                    for t in range(T):
                        last = te.matmul(misc[:, cols * t:cols * t + cols], moving[:, 128 * t:128 * t + 128],
                                         weight[:], start=True, stop=True)
                last.then_inc(misc_full, 1)

            for step in SCHEDULE:
                kind, b, k = step
                use = MISC.get(step, 0)
                misc = misc_bank(use)
                if kind == "warm":
                    if ("xpeak", B - 1, len(XPEAKS) - 1) in SCHEDULE[:b]:
                        pe.wait_ge(peak_taken, PEAK[("xpeak", B - 1, len(XPEAKS) - 1)])
                    else:
                        wait_cleared(pe, "ones_b")
                    for _ in range(k):
                        te.matmul(peak_ps[:, 0], ones_b[:, 0:128], ones_b[:], start=True, stop=True)
                elif kind == "context_keys":
                    pe.wait_ge(rest_loaded, 16 * N_REST)
                    misc_free(use)
                    te.matmul(misc[:, 0:B * S2], xwk_s[:], ctx_s[:], start=True, stop=True).then_inc(misc_full, 1)
                elif kind == "context_values":
                    misc_free(use)
                    te.matmul(misc[0:S2, 0:D], ctx_s[:, S2 * b:S2 * b + S2], xwv_s[:], start=True, stop=True
                              ).then_inc(misc_full, 1)
                elif kind == "turn_x":
                    i = NORM[("ln_norm", b, k)]
                    if b == 0 and k == 0:
                        wait_cleared(pe, "ident")
                    pe.wait_ge(norm_ready, i)
                    misc_free(use)
                    for t in range(T):
                        last = te.transpose(misc[:, 128 * t:128 * t + 128], normed[:, i % 2, t], ident[:])
                    last.then_inc(misc_full, 1)
                elif kind == "project_q":
                    wait_misc_taken(pe, MISC[("turn_x", b, 0)])
                    if b == 0:
                        pe.wait_ge(first_loaded, 16 * len(FIRST))
                    product(wq_s, normed_t[0][:], use)
                elif kind == "project_k":
                    product(wk_s, normed_t[0][:], use)
                elif kind == "project_v":
                    product(wv_s, normed_t[0], use, tiles=True)
                elif kind == "project_xq":
                    wait_misc_taken(pe, MISC[("turn_x", b, 1)])
                    product(xwq_s, normed_t[1][:], use)
                elif kind == "gate":
                    wait_misc_taken(pe, MISC[("turn_x", b, 2)])
                    product(gate_w_s, normed_t[2], use, tiles=True)
                elif kind == "peak":
                    f, u = k
                    t, heads = PEAKS[u]
                    width = 128 * (t + 1)
                    if u == 0:
                        if b == 0:
                            wait_cleared(pe, "causal")
                        pe.wait_ge(stacked["q"][b % 2], 16 * STACK_DMAS * (b // 2 + 1))
                        pe.wait_ge(stacked["k"][b % 2], 16 * STACK_DMAS * (b // 2 + 1))
                    peak_free(step)
                    bank = peak_bank(step)
                    n = sum(1 if s is not None else 2 for _, s in heads)
                    diagonal = bank[:, 0:n * width].rearrange("p (h k) -> p h k", h=n)[:, :, width - 128:width]
                    te.matmul(diagonal, ident_b[:], causal[:, 0:n], start=True, stop=False, skip_group_check=True)
                    for i, (p, s) in enumerate(heads):
                        q = q_stack[0:MAX_ROW, b % 2, 4 * f + p, 128 * t:128 * t + 128]
                        if s is None:
                            keys = k_stack[0:MAX_ROW, b % 2, :, 4 * f + p, 0:width]
                            dst = bank[:, 2 * width * i:2 * width * (i + 1)].rearrange("p (s k) -> p s k", s=2)
                        else:
                            keys = k_stack[0:MAX_ROW, b % 2, s, 4 * f + p, 0:width]
                            dst = bank[:, 0:width]
                        last = te.matmul(dst, q, keys, start=False, stop=(i == len(heads) - 1), skip_group_check=True)
                    last.then_inc(peak_full, 1)
                elif kind == "xpeak":
                    t, h, n = XPEAKS[k]
                    if k == 0:
                        pe.wait_ge(stacked["x"][b % 2], 16 * STACK_DMAS * (b // 2 + 1))
                        pe.wait_ge(xk_stacked, 16 * N_XK)
                    peak_free(step)
                    for i in range(n):
                        p, s = (h + i) // 2, (h + i) % 2
                        last = te.matmul(peak_bank(step)[:, S2 * i:S2 * i + S2],
                                         xq_stack[0:XMAX_ROW, p, 128 * t:128 * t + 128],
                                         xk_stack[0:XMAX_ROW, s, p, S2 * b:S2 * b + S2], start=True, stop=True)
                    last.then_inc(peak_full, 1)
                elif kind in ("turn_peaks", "turn_xpeaks"):
                    self_attention = kind == "turn_peaks"
                    src = peak_parts[:, k] if self_attention else xpeak_parts[:]
                    rows = 24 if self_attention else 48
                    pe.wait_ge(peaks_split if self_attention else xpeaks_split, 2 * b + k + 1 if self_attention else b + 1)
                    misc_free(use)
                    for t in range(T):
                        last = te.transpose(misc[0:rows, 64 * t:64 * t + 64].bitcast(BF16),
                                            src[:, t].rearrange("p s i a -> p (s i a)"), ident_b[:])
                    last.then_inc(misc_full, 1)
                elif kind == "scores":
                    grp, u = k
                    if (b, grp, u) == (0, 0, 0):
                        pe.wait_ge(ones_stacked, 16 * 4)
                        pe.wait_ge(cleared_later, 2)
                    if u == 0 and grp % 2 == 0:
                        pe.wait_ge(max_stacked[grp // 2], 32 * (b + 1))
                    unit_free(step)
                    for col, j, kt in SCORES[u]:
                        h = 4 * grp + j
                        p, s = h // 2, h % 2
                        n = S - 128 * kt
                        last = te.matmul(unit_bank(step)[:, col:col + n], k_stack[0:ROWS, b % 2, s, p, 128 * kt:128 * kt + 128],
                                         q_stack[0:ROWS, b % 2, p, 128 * kt:S], start=True, stop=True)
                    last.then_inc(unit_full, 1)
                elif kind == "values":
                    grp, v = k
                    tiles, u = VALUES[v]
                    pe.wait_ge(causal_done, 5 * (4 * b + grp) + u + 1)
                    if v == 0:
                        if MIX[("take_mix", b, grp)] > 1:
                            pe.wait_ge(mix_taken, MIX[("take_mix", b, grp)] - 1)
                        wait_misc_taken(pe, MISC[("project_v", b, 0)])
                    for kt in tiles:
                        for j in range(4):
                            unit, col = PLACE[(kt, j)]
                            last = te.matmul(mix_ps[32 * j:32 * j + VW, 128 * kt:S], v_s[:, b % 2, kt, 4 * grp + j],
                                             probs[:, grp % 2, unit, col:col + S - 128 * kt],
                                             start=(kt == 0), stop=(kt == 2), skip_group_check=True)
                    last.then_inc(values_done, 1)
                elif kind == "xscores":
                    if k == 0:
                        pe.wait_ge(xmax_stacked, 32 * (b + 1))
                    unit_free(step)
                    te.matmul(unit_bank(step)[0:S2], xk_stack[0:XROWS, k % 2, k // 2, S2 * b:S2 * b + S2],
                              xq_stack[0:XROWS, k // 2], start=True, stop=True).then_inc(unit_full, 1)
                elif kind == "xvalues":
                    for h in range(4 * k, 4 * k + 4):
                        wait_unit_taken(pe, ("xscores", b, h))
                    misc_free(use)
                    for j in range(4):
                        last = te.matmul(misc[32 * j:32 * j + VW, :], xv_s[0:S2, b, 4 * k + j],
                                         xprobs[0:S2, (H * b + 4 * k + j) % XPROBS], start=True, stop=True)
                    last.then_inc(misc_full, 1)
                elif kind in ("mix", "xmix"):
                    i = int(kind == "xmix")
                    if i:
                        wait_misc_taken(pe, MISC[("xvalues", b, k)])
                    else:
                        pe.wait_ge(mix_taken, MIX[("take_mix", b, k)])
                    misc_free(use)
                    for t in range(T):
                        last = te.transpose(misc[:, 128 * t:128 * t + 128], mix_t[:, i, 128 * t:128 * t + 128],
                                            ident[:])
                    last.then_inc(misc_full, 1)
                elif kind == "turn_mix":
                    wait_misc_taken(pe, MISC[("xmix" if k else "mix", b, 3)])
                    misc_free(use)
                    for t in range(T):
                        last = te.transpose(misc[:, 128 * t:128 * t + 128], mixed[:, k, t], ident[:])
                    last.then_inc(misc_full, 1)
                elif kind == "add_attention":
                    wait_misc_taken(pe, MISC[("turn_mix", b, k)])
                    product(xwo_s if k else wp_s, mixed_t[:, k], use, tiles=True)
                elif kind == "turn_gate":
                    pe.wait_ge(comb_ready, b + 1)
                    misc_free(use)
                    te.transpose(misc[0:T * E, 0:128], g["comb"][:].rearrange("p t e -> p (t e)"), ident[:]
                                 ).then_inc(misc_full, 1)
                elif kind == "expert_bias":
                    wait_misc_taken(pe, MISC[("turn_gate", b, 0)])
                    if b == 0:
                        pe.wait_ge(biases_loaded, 16 * T)
                    misc_free(use)
                    for t in range(T):
                        last = te.matmul(misc[:, D * t:D * t + D], comb_t[:], expert_b_s[:, t], start=True, stop=True)
                    last.then_inc(misc_full, 1)
                elif kind == "expert":
                    unit_free(step)
                    t, half = divmod(k, 2)
                    te.matmul(unit_bank(step), normed_t[2][:, 128 * t:128 * t + 128],
                              expert_w_s[:, 4 * half:4 * half + 4].rearrange("d e f -> d (e f)"),
                              start=True, stop=True).then_inc(unit_full, 1)


def kernel(**inputs):
    import concourse.bacc as bacc
    from concourse.bass_utils import run_bass_kernel_spmd

    a = {k: np.asarray(v) for k, v in inputs.items()}

    def by_slot(w):
        return w.reshape(*w.shape[:-1], PAIRS, 2, DH).swapaxes(-3, -2).swapaxes(-2, -1).reshape(w.shape)

    arrays = {
        "x": a["x"],
        "ctx_t": a["ctx_1024"].transpose(2, 0, 1).reshape(D, B * S2),
        "mask": a["mask_Bx1x1xS2_bk0"].reshape(B * S2),
        "wq": by_slot(a["L0_attn_Wq"]), "bq": by_slot(a["L0_attn_bq"]).reshape(D, 1),
        "wk": by_slot(a["L0_attn_Wk"]), "bk": by_slot(a["L0_attn_bk"]).reshape(D, 1),
        "wv": a["L0_attn_Wv"], "bv": a["L0_attn_bv"],
        "wp": a["L0_attn_Wp"], "bp": a["L0_attn_bp"],
        "xwq": by_slot(a["L0_xattn_Wq"].T), "xwk": by_slot(a["L0_xattn_Wk"].T),
        "xwv": a["L0_xattn_Wv"].T, "xwo": a["L0_xattn_Wo"].T,
        "gate_w": a["L0_ffn_gate_W"], "gate_b": a["L0_ffn_gate_b"],
        "expert_w": a["L0_ffn_expert_W"], "expert_b": a["L0_ffn_expert_b"],
    }
    arrays = {k: np.ascontiguousarray(v) for k, v in arrays.items()}
    nc = bacc.Bacc("TRN2", target_bir_lowering=False, num_devices=1)
    args = [nc.dram_tensor(f"in_{k}", v.shape, mybir.dt.from_np(v.dtype), kind="ExternalInput").ap()
            for k, v in arrays.items()]
    out = nc.dram_tensor("out", (B, S, D), F32, kind="ExternalOutput").ap()
    names = list(arrays)
    decoder_layer(nc, **dict(zip(names, args)), out=out)
    r = run_bass_kernel_spmd(nc, [{f"in_{k}": v for k, v in arrays.items()}], core_ids=[0])
    return r.results[0]["out"]
```
